# Optimizing a Trainium2 kernel written in Bass

```python
import numpy as np
import jax
import jax.numpy as jnp

def _softmax(x, axis=-1):
    return jax.nn.softmax(x, axis=axis)

def _gelu(x):
    return jax.nn.gelu(x, approximate=True)

def _silu(x):
    return jax.nn.silu(x)

def _sigmoid(x):
    return jax.nn.sigmoid(x)

def _layernorm(x, axis=-1, eps=1e-05):
    m = jnp.mean(x, axis=axis, keepdims=True)
    v = jnp.var(x, axis=axis, keepdims=True)
    return (x - m) / jnp.sqrt(v + eps)

def _scatter_add(tgt, idx, src, axis=0):
    return tgt.at[idx].add(src)

def _segment_sum(src, seg, n):
    return jax.ops.segment_sum(src, seg, n)
kernel_name = 'mk_seq_postln_d1_jaxref_r4_21fde0'

def setup_inputs(seed: int=0):
    np.random.seed(seed)
    _w = jnp.asarray

    def _L0_attn_setup():
        import jax, jax.numpy as jnp
        import numpy as np
        D_MODEL = 512
        NUM_HEADS = 16
        HEAD_DIM = D_MODEL // NUM_HEADS

        def _rotary(x, head_dim):
            T = x.shape[-2]
            pos = jnp.arange(T, dtype=jnp.float32)[:, None]
            dim = jnp.arange(head_dim // 2, dtype=jnp.float32)[None, :]
            angle = pos * (1.0 / jnp.power(10000.0, 2.0 * dim / head_dim))
            cos = jnp.cos(angle)
            sin = jnp.sin(angle)
            x1 = x[..., :head_dim // 2]
            x2 = x[..., head_dim // 2:]
            return jnp.concatenate([x1 * cos - x2 * sin, x2 * cos + x1 * sin], axis=-1)
        key = jax.random.key(seed)
        ks = jax.random.split(key, 9)
        B, T, D, H, HD = (2, 512, D_MODEL, NUM_HEADS, HEAD_DIM)
        s = 1.0 / np.sqrt(D)
        return {'x': jax.random.normal(ks[0], (B, T, D), jnp.float32), 'Wq': jax.random.normal(ks[1], (D, D), jnp.float32) * s, 'bq': jnp.zeros((D,), jnp.float32), 'Wk': jax.random.normal(ks[2], (D, HD), jnp.float32) * s, 'bk': jnp.zeros((HD,), jnp.float32), 'Wv': jax.random.normal(ks[3], (D, HD), jnp.float32) * s, 'bv': jnp.zeros((HD,), jnp.float32), 'Wo': jax.random.normal(ks[4], (D, D), jnp.float32) * s, 'bo': jnp.zeros((D,), jnp.float32)}
    _L0_attn_in = _L0_attn_setup()

    def _L0_ffn_setup():
        import jax, jax.numpy as jnp
        import numpy as np
        EPS = 1e-08

        def _quantize(w):
            gamma = jnp.mean(jnp.abs(w))
            return jnp.clip(jnp.round(w / (gamma + EPS)), -1.0, 1.0)

        def _bitlinear(x, w):
            return jnp.matmul(x, _quantize(w).T)
        key = jax.random.key(seed)
        k1, k2, k3, k4 = jax.random.split(key, 4)
        d, h = (512, 1408)
        x = jax.random.normal(k1, (4, 512, d), dtype=jnp.float32)
        w1 = jax.random.normal(k2, (h, d), dtype=jnp.float32)
        w2 = jax.random.normal(k3, (h, d), dtype=jnp.float32)
        w3 = jax.random.normal(k4, (d, h), dtype=jnp.float32)
        return {'x': x, 'w1': w1, 'w2': w2, 'w3': w3}
    _L0_ffn_in = _L0_ffn_setup()
    _d = {'L0_attn_x': _L0_attn_in['x'], 'L0_attn_Wq': _L0_attn_in['Wq'], 'L0_attn_bq': _L0_attn_in['bq'], 'L0_attn_Wk': _L0_attn_in['Wk'], 'L0_attn_bk': _L0_attn_in['bk'], 'L0_attn_Wv': _L0_attn_in['Wv'], 'L0_attn_bv': _L0_attn_in['bv'], 'L0_attn_Wo': _L0_attn_in['Wo'], 'L0_attn_bo': _L0_attn_in['bo'], 'L0_ffn_w1': _L0_ffn_in['w1'], 'L0_ffn_w2': _L0_ffn_in['w2'], 'L0_ffn_w3': _L0_ffn_in['w3']}
    _x0 = _d['L0_attn_x']
    _d['L0_attn_x'] = jax.random.normal(jax.random.fold_in(jax.random.key(seed), 1), (4, 512, 512), dtype=_x0.dtype)
    del _x0
    return _d

def reference(L0_attn_x, L0_attn_Wq, L0_attn_bq, L0_attn_Wk, L0_attn_bk, L0_attn_Wv, L0_attn_bv, L0_attn_Wo, L0_attn_bo, L0_ffn_w1, L0_ffn_w2, L0_ffn_w3):

    def _L0_attn_ref(x, Wq, bq, Wk, bk, Wv, bv, Wo, bo):
        import jax, jax.numpy as jnp
        import numpy as np
        D_MODEL = 512
        NUM_HEADS = 16
        HEAD_DIM = D_MODEL // NUM_HEADS

        def _rotary(x, head_dim):
            T = x.shape[-2]
            pos = jnp.arange(T, dtype=jnp.float32)[:, None]
            dim = jnp.arange(head_dim // 2, dtype=jnp.float32)[None, :]
            angle = pos * (1.0 / jnp.power(10000.0, 2.0 * dim / head_dim))
            cos = jnp.cos(angle)
            sin = jnp.sin(angle)
            x1 = x[..., :head_dim // 2]
            x2 = x[..., head_dim // 2:]
            return jnp.concatenate([x1 * cos - x2 * sin, x2 * cos + x1 * sin], axis=-1)
        B, T, D = x.shape
        H, HD = (NUM_HEADS, HEAD_DIM)
        q = (x @ Wq + bq).reshape(B, T, H, HD).transpose(0, 2, 1, 3)
        k = (x @ Wk + bk)[:, None]
        v = (x @ Wv + bv)[:, None]
        q = _rotary(q, HD)
        k = _rotary(k, HD)
        scores = jnp.einsum('bhqd,bhkd->bhqk', q, jnp.broadcast_to(k, (B, 1, T, HD))) / jnp.sqrt(jnp.float32(HD))
        attn = jax.nn.softmax(scores, axis=-1)
        ctx = jnp.einsum('bhqk,bhkd->bhqd', attn, jnp.broadcast_to(v, (B, 1, T, HD)))
        ctx = ctx.transpose(0, 2, 1, 3).reshape(B, T, D)
        return ctx @ Wo + bo

    def _L0_ffn_ref(x, w1, w2, w3):
        import jax, jax.numpy as jnp
        import numpy as np
        EPS = 1e-08

        def _quantize(w):
            gamma = jnp.mean(jnp.abs(w))
            return jnp.clip(jnp.round(w / (gamma + EPS)), -1.0, 1.0)

        def _bitlinear(x, w):
            return jnp.matmul(x, _quantize(w).T)
        x1 = _bitlinear(x, w1)
        x2 = _bitlinear(x, w2)
        hidden = jax.nn.sigmoid(x1) * x2
        return _bitlinear(hidden, w3)
    x = L0_attn_x
    x = _layernorm(x + _L0_attn_ref(x, L0_attn_Wq, L0_attn_bq, L0_attn_Wk, L0_attn_bk, L0_attn_Wv, L0_attn_bv, L0_attn_Wo, L0_attn_bo), axis=-1)
    x = _layernorm(x + _L0_ffn_ref(x, L0_ffn_w1, L0_ffn_w2, L0_ffn_w3), axis=-1)
    return x

_drawn_inputs = setup_inputs


def setup_inputs(seed=0):
    import zlib

    import numpy as np

    out = dict(_drawn_inputs(seed))
    spreads = {'L0_attn_bq': (0.0, 0.553),
     'L0_attn_bk': (0.0, 0.764),
     'L0_attn_bv': (0.0, 0.1),
     'L0_attn_bo': (0.0, 0.1)}
    factors = {}
    for name, (base, spread) in spreads.items():
        noise = np.random.default_rng([zlib.crc32(name.encode()), seed]).standard_normal(out[name].shape)
        drawn = base * np.exp(spread * noise) if base else spread * noise
        out[name] = jnp.asarray(drawn.astype(out[name].dtype))
    for name, factor in factors.items():
        out[name] = (out[name] * factor).astype(out[name].dtype)
    return out
```

```python
from contextlib import ExitStack

import numpy as np

import concourse.bass as bass
from concourse import mybir

F32 = mybir.dt.float32
F32R = mybir.dt.float32r
F16 = mybir.dt.float16
ALU = mybir.AluOpType
ACT = mybir.ActivationFunctionType
AX = mybir.AxisListType
RADD = bass.bass_isa.ReduceOp.add

P = 128
B, T, D, H, F = 4, 512, 512, 16, 1408
HD = D // H
DT = D // P
TT = T // P
HG = H * HD // P
HPG = H // HG
FT = F // P
SCALE = float(HD) ** -0.5
LN_EPS = 1e-5
Q_EPS = 1e-8
H_SCALE = 32.0
G_SCALE = 2 * H_SCALE
PTR = HPG
QR = 2
PIECES = 4
SR = 3
UNITS = ["q0", "k", "q1", "q2", "q3"]
BESIDE = (["up0", "up1", "up2", "up3", "q2", "up4", "up5", "up6", "q3"]
          + [f"up{f}" for f in range(7, FT)] + ["", "dn0", "dn1"])
BESIDE += [""] * (H + 1 - len(BESIDE))


ABS_AT = [0, 2, 10]
QUANTISE_AT = list(range(1, 9)) + list(range(11, 15))


def bank_uses(bank):
    uses = ["q0", "q1", "ht0", "ht2"] if bank == "a" else ["k", "vp", "ht1", "vf", "ht3"]
    for h in range(H + 1):
        if h % HPG == 1 and h > HPG and bank == "a":
            uses.append(f"r{h // HPG - 1}")
        use = BESIDE[h]
        if use[:2] == "up" or (use[:1] == "q" and bank == "a"):
            uses.append(use)
        elif use[:2] == "dn" and (int(use[2:]) % 2 == 0) == (bank == "a"):
            uses.append(use)
    uses += ["dn2", f"r{HG - 1}", "wo0", "wo2"] if bank == "a" else ["dn3", "wo1", "wo3"]
    return uses


def at_use(bank, period, use):
    uses = bank_uses(bank)
    early = [u for u in uses if u[:2] not in ("ht", "up", "dn")]
    if isinstance(period, int) and period == 0:
        return early.index(use) + 1
    if isinstance(period, int) and period == B:
        late = [u for u in uses if u[:2] in ("ht", "up", "dn")]
        return len(early) + (B - 1) * len(uses) + late.index(use) + 1
    return len(early) + (period - 1) * len(uses) + uses.index(use) + 1


def layer(nc, xT, x, wq, wk, wv, wo, bq, bk, bv, bo, w1, w2, w3, cos, sin, ident, eye4, out):
    with ExitStack() as ctx:
        def sb(name, shape, dt=F32):
            return ctx.enter_context(nc.sbuf_tensor(name, shape, dt))

        def sem(name):
            return ctx.enter_context(nc.semaphore(name))

        wq_sb = sb("wq_sb", [P, DT, D])
        wo_sb = sb("wo_sb", [P, HG, D])
        wk_sb = sb("wk_sb", [P, DT, HPG, HD])
        wkv_ld = sb("wkv_ld", [P, 2, DT, HD])
        q1 = sb("q1", [P, DT * F], F16)
        q2 = sb("q2", [P, DT * F], F16)
        q3 = sb("q3", [P, FT * D], F16)
        bias = sb("bias", [P, HG + 1])
        bv_sb = sb("bv_sb", [P, HD])
        bo_sb = sb("bo_sb", [P, D])
        cos_sb = sb("cos_sb", [P, T])
        sin_sb = sb("sin_sb", [P, T])
        id_sb = sb("id_sb", [P, P])
        eye4_sb = sb("eye4_sb", [P, HD])
        xT_sb = sb("xT_sb", [P, DT, T])
        late = sb("late", [P, FT * T + 3 * DT * T])
        raw = sb("raw", [P, 2, T])
        rot = sb("rot", [P, 2, T])
        th = sb("th", [P, T])
        hi = sb("hi", [P, T], F32R)
        lo = sb("lo", [P, T], F32R)
        q_st = sb("q_st", [P, QR * HPG, T], F32R)
        k_st = sb("k_st", [P, T], F32R)
        v_sb = sb("v_sb", [P, TT, HD])
        p_sb = sb("p_sb", [P, 2, TT, T])
        pt_sb = sb("pt_sb", [P, PTR, TT, T])
        sh_sb = sb("sh_sb", [P, 2 * SR])
        sums = sb("sums", [P, H, TT])
        rc = sb("rc", [P, H, TT])
        rexp = sb("rexp", [P, TT, HPG, HD])
        rT = sb("rT", [P, T])
        cx = sb("cx", [P, HG, T])
        stat = sb("stat", [P, 2, TT, 6])
        mv = sb("mv", [P, 2, TT, 2])
        rstd = sb("rstd", [P, 2, TT])
        nhalf = sb("nhalf", [P, 1])
        asum = sb("asum", [P, 3])
        atot = sb("atot", [P, 3])
        thr = sb("thr", [P, 3, 2])

        gT = late[:, 0:FT * T].bitcast(F16).rearrange("p (s f t) -> p s f t", s=2, f=FT)
        hT = late[:, FT * T:FT * T + DT * T].bitcast(F16).rearrange("p (s k t) -> p s k t", s=2, k=DT)
        h_sb = late[:, FT * T + DT * T:FT * T + 2 * DT * T].rearrange("p (t d) -> p t d", t=TT)
        xb = late[:, FT * T + 2 * DT * T:FT * T + 3 * DT * T].rearrange("p (t d) -> p t d", t=TT)
        vp_sb = rexp[:, :, :, :].rearrange("p t j d -> p (t j d)")
        stage = [late[:, n * DT * F:(n + 1) * DT * F] for n in (0, 1, 0)]
        q1v = q1[:, :].rearrange("p (k f) -> p k f", k=DT)
        q2v = q2[:, :].rearrange("p (k f) -> p k f", k=DT)
        q3v = q3[:, :].rearrange("p (f d) -> p f d", f=FT)

        def bank(name):
            return ctx.enter_context(nc.psum_tensor(name, [P, 512], F32))

        s_ps = [bank(f"s_ps{n}") for n in range(SR)]
        t_ps = [bank(f"t_ps{n}") for n in range(2)]
        c_ps = bank("c_ps")
        a_ps = bank("a_ps")
        b_ps = bank("b_ps")

        w_proj = sem("w_proj")
        w_late = sem("w_late")
        w_ffn = [sem(f"w_ffn{n}") for n in range(3)]
        abs_summed = sem("abs_summed")
        abs_total = sem("abs_total")
        thr_step = sem("thr_step")
        compared = sem("compared")
        quantised = sem("quantised")
        nhalf_set = sem("nhalf_set")
        bias_scaled = sem("bias_scaled")
        wk_repeated = sem("wk_repeated")
        xT_in = sem("xT_in")
        x_in = sem("x_in")
        bo_added = sem("bo_added")
        a_filled = sem("a_filled")
        a_drained = sem("a_drained")
        b_filled = sem("b_filled")
        b_drained = sem("b_drained")
        cos_done = sem("cos_done")
        swapped = sem("swapped")
        sin_done = sem("sin_done")
        rotated = sem("rotated")
        hi_done = sem("hi_done")
        lo_done = sem("lo_done")
        k_ready = sem("k_ready")
        q_in = [sem(f"q_in{g}") for g in range(HG)]
        scored = sem("scored")
        maxed = sem("maxed")
        expd = sem("expd")
        transposed = sem("transposed")
        pt_act = sem("pt_act")
        pt_dve = sem("pt_dve")
        recip_done = sem("recip_done")
        rexp_done = sem("rexp_done")
        ctx_filled = sem("ctx_filled")
        ctx_done = sem("ctx_done")
        stat_done = sem("stat_done")
        mv_done = sem("mv_done")
        eps_added = sem("eps_added")
        rstd_done = sem("rstd_done")
        normed = sem("normed")
        h_hi = sem("h_hi")
        h_lo = sem("h_lo")
        gated = sem("gated")
        g_hi = sem("g_hi")
        g_lo = sem("g_lo")
        stored = sem("stored")
        stood = sem("stood")

        def stand(engine):
            engine.sem_inc(stood, 1)

        def ain(b, use):
            return at_use("a", b, use)

        def bin_(b, use):
            return at_use("b", b, use)

        def wide(n):
            return (a_ps, a_filled, a_drained, ain) if n % 2 == 0 else (b_ps, b_filled, b_drained, bin_)

        def piece(ap, c):
            return ap[:, c * DT * F // PIECES:(c + 1) * DT * F // PIECES]

        block = ctx.enter_context(nc.Block())


        @block.sync
        def _(sp):
            sp.dma_start(wq_sb[:, :, :], wq.rearrange("(k p) n -> p k n", p=P)).then_inc(w_proj, 16)

            def stack(b, g):
                sp.wait_ge(lo_done, b * len(UNITS) + UNITS.index(f"q{g}") + 1)
                for j in range(HPG):
                    for r in range(4):
                        half = (hi, lo)[r % 2]
                        sp.dma_start(q_st[HD * r:HD * (r + 1), g % QR * HPG + j, :].bitcast(F32),
                                     half[HD * j:HD * (j + 1), :].bitcast(F32)).then_inc(q_in[g], 16)

            def period(b):
                first = isinstance(b, int)
                sp.dma_start(xT_sb[:, :, :].rearrange("p k t -> p (k t)"), xT[b, :, :]).then_inc(xT_in, 16)
                if first:
                    sp.dma_start(stage[0], w1).then_inc(w_ffn[0], 16)
                    sp.dma_start(stage[1], w2).then_inc(w_ffn[1], 16)
                stack(b, 0)
                stack(b, 1)
                if not first:
                    sp.wait_ge(normed, (b * 2 - 1) * TT)
                    stand(sp)
                    sp.dma_start(xb, x[b, :, :].rearrange("(t p) d -> p t d", p=P)).then_inc(x_in, 16)
                sp.wait_ge(scored, (b * H + HPG) * TT)
                stand(sp)
                stack(b, 2)
                if first:
                    sp.wait_ge(quantised, PIECES)
                    sp.dma_start(stage[2], w3).then_inc(w_ffn[2], 16)
                sp.wait_ge(scored, (b * H + 2 * HPG) * TT)
                stand(sp)
                stack(b, 3)
                if first:
                    sp.wait_ge(quantised, 2 * PIECES)
                    sp.dma_start(xb, x[b, :, :].rearrange("(t p) d -> p t d", p=P)).then_inc(x_in, 16)
                sp.wait_ge(a_filled, ain(b, "q3"))
                stand(sp)

            period(0)
            with sp.Fori(1, B) as b:
                period(b)

        @block.gpsimd
        def _(pool):
            pool.memset(nhalf[:, :], -0.5).then_inc(nhalf_set, 1)
            pool.wait_ge(nhalf_set, 1)

            def cosines(b, name):
                u = UNITS.index(name)
                if name == "k":
                    pool.wait_ge(b_drained, bin_(b, "k"))
                else:
                    pool.wait_ge(a_drained, ain(b, name))
                pool.wait_ge(rotated, b * len(UNITS) + u)
                pool.tensor_tensor(rot[:, 0, :], raw[:, u % 2, :], cos_sb[:, :], ALU.mult).then_inc(cos_done, 1)

            def total(n):
                pool.wait_ge(abs_summed, n + 1)
                pool.partition_all_reduce(atot[:, n:n + 1], asum[:, n:n + 1], P, RADD).then_inc(abs_total, 1)

            def rstds(c, ln):
                for t in range(TT):
                    n = (c * 2 + ln) * TT + t
                    pool.wait_ge(mv_done, n + 1)
                    stand(pool)
                    pool.tensor_scalar(rstd[:, ln, t:t + 1], mv[:, ln, t, 1:2], LN_EPS, None,
                                       ALU.add).then_inc(eps_added, 1)
                    pool.wait_ge(eps_added, n + 1)
                    pool.tensor_tensor(rstd[:, ln, t:t + 1], rstd[:, ln, t:t + 1], nhalf[:, :],
                                       ALU.pow).then_inc(rstd_done, 1)

            def store(c):
                for t in range(TT):
                    pool.wait_ge(normed, (c * 2 + 1) * TT + t + 1)
                    stand(pool)
                    pool.dma_start(out[c, t * P:(t + 1) * P, :], h_sb[:, t, :]).then_inc(stored, 16)

            def period(b):
                first = isinstance(b, int)
                cosines(b, "q0")
                cosines(b, "k")
                cosines(b, "q1")
                if first:
                    total(0)
                    total(1)
                cosines(b, "q2")
                cosines(b, "q3")
                if first:
                    total(2)
                pool.wait_ge(x_in, (b + 1) * 16)
                for t in range(TT):
                    pool.tensor_tensor(xb[:, t, :], xb[:, t, :], bo_sb[:, :], ALU.add).then_inc(bo_added, 1)
                if not first:
                    rstds(b - 1, 1)
                    store(b - 1)
                rstds(b, 0)

            pool.wait_ge(w_late, 16 * 5)
            period(0)
            with pool.Fori(1, B) as b:
                period(b)
            rstds(B - 1, 1)
            store(B - 1)
            pool.wait_ge(stored, B * TT * 16)

        @block.scalar
        def _(act):
            act.dma_start(wkv_ld[:, 0, :, :].rearrange("p k d -> p (k d)"), wk).then_inc(w_proj, 16)
            act.dma_start(wkv_ld[:, 1, :, :].rearrange("p k d -> p (k d)"), wv).then_inc(w_proj, 16)
            act.dma_start(bias[:, 0:HG], bq).then_inc(w_proj, 16)
            for j in range(HPG):
                act.dma_start(bias[HD * j:HD * (j + 1), HG:HG + 1], bk).then_inc(w_proj, 16)
            act.dma_start(cos_sb[:, :], cos).then_inc(w_proj, 16)
            act.dma_start(sin_sb[:, :], sin).then_inc(w_proj, 16)
            act.dma_start(bv_sb[:, :], bv.partition_broadcast(P)).then_inc(w_late, 16)
            act.dma_start(bo_sb[:, :], bo.partition_broadcast(P)).then_inc(w_late, 16)
            act.dma_start(id_sb[:, :], ident).then_inc(w_late, 16)
            act.dma_start(eye4_sb[:, :], eye4).then_inc(w_late, 16)
            act.dma_start(wo_sb[:, :, :], wo.rearrange("(k p) n -> p k n", p=P)).then_inc(w_late, 16)

            def unit(b, name):
                u = UNITS.index(name)
                seen = b * len(UNITS) + max(u - 1, 0)
                act.wait_ge(cos_done, seen)
                act.wait_ge(swapped, seen)
                if name == "k":
                    act.wait_ge(b_filled, bin_(b, name))
                    act.activation(raw[:, u % 2, :], b_ps[:, :], ACT.Identity,
                                   bias=bias[:, HG:HG + 1]).then_inc(b_drained, 1)
                else:
                    g = int(name[1:])
                    act.wait_ge(a_filled, ain(b, name))
                    act.activation(raw[:, u % 2, :], a_ps[:, :], ACT.Identity, bias=bias[:, g:g + 1],
                                   scale=-SCALE).then_inc(a_drained, 1)

            def h_high(b, t):
                ps, filled, drained, at = wide(t)
                act.wait_ge(filled, at(b, f"ht{t}"))
                act.activation(hT[:, 0, :, t * P:(t + 1) * P], ps[:, :].rearrange("p (k t) -> p k t", k=DT),
                               ACT.Copy, scale=H_SCALE).then_inc(h_hi, 1)

            def tanh(b, f):
                act.wait_ge(a_filled, ain(b, f"up{f}"))
                if f:
                    act.wait_ge(gated, (b - 1) * FT + f)
                act.activation(th[:, :], a_ps[:, :], ACT.Tanh, scale=0.5 / H_SCALE).then_inc(a_drained, 1)

            def g_high(b, f):
                act.wait_ge(gated, (b - 1) * FT + f + 1)
                act.activation(gT[:, 0, f, :], b_ps[:, :], ACT.Copy).then_inc(g_hi, 1)

            def exps(b, h, t):
                n = h * TT + t
                act.wait_ge(maxed, b * H * TT + n + 1)
                if t == 0:
                    act.wait_ge(transposed, b * H * TT + max(h - 1, 0) * TT)
                act.activation(p_sb[:, h % 2, t, :], s_ps[n % SR][:, :], ACT.Exp,
                               bias=sh_sb[:, n % (2 * SR):n % (2 * SR) + 1], scale=-1.0,
                               accum_out=sums[:, h, t:t + 1]).then_inc(expd, 1)

            def move(b, h, k):
                act.wait_ge(transposed, b * H * TT + h * TT + k + 1)
                if h >= PTR:
                    act.wait_ge(ctx_filled, b * HG + (h - PTR) // HPG + 1)
                act.activation(pt_sb[:, h % PTR, k, :], t_ps[k % 2][:, :], ACT.Copy).then_inc(pt_act, 1)

            def norm_row(b, g):
                act.wait_ge(a_filled, ain(b, f"r{g}"))
                act.wait_ge(ctx_done, b * HG + g)
                act.activation(rT[:, :], a_ps[:, :], ACT.Copy).then_inc(a_drained, 1)

            def period(b):
                first = isinstance(b, int)
                unit(b, "q0")
                unit(b, "k")
                act.wait_ge(b_filled, bin_(b, "vp"))
                act.activation(vp_sb, b_ps[:, :], ACT.Copy).then_inc(b_drained, 1)
                unit(b, "q1")
                if not first:
                    for t in range(TT):
                        h_high(b, t)
                owed = ""
                for h in range(H + 1):
                    use = BESIDE[h]
                    if first and use[:1] != "q":
                        use = ""
                    if h < H:
                        exps(b, h, 0)
                        exps(b, h, 1)
                    if owed:
                        g_high(b, int(owed[2:]))
                    owed = use if use[:2] == "up" else ""
                    if h % HPG == 1 and h > HPG:
                        norm_row(b, h // HPG - 1)
                    if h < H:
                        exps(b, h, 2)
                    if use[:2] == "up":
                        tanh(b, int(use[2:]))
                    if h >= 1:
                        move(b, h - 1, 0)
                    if use[:1] == "q":
                        unit(b, use)
                    if h < H:
                        exps(b, h, 3)
                    if h >= 1:
                        move(b, h - 1, 2)
                    if first and h in ABS_AT:
                        n = ABS_AT.index(h)
                        act.wait_ge(w_ffn[n], 16)
                        act.activation((q1, q2, q3)[n][:, :], stage[n], ACT.Abs,
                                       accum_out=asum[:, n:n + 1]).then_inc(abs_summed, 1)
                norm_row(b, HG - 1)

            act.wait_ge(bias_scaled, 1)
            period(0)
            with act.Fori(1, B) as b:
                period(b)
            for t in range(TT):
                h_high(B, t)
            for f in range(FT):
                tanh(B, f)
                g_high(B, f)

        @block.vector
        def _(dve):
            dve.wait_ge(w_proj, 16 * 10)
            dve.tensor_scalar(bias[:, 0:HG], bias[:, 0:HG], -SCALE, None, ALU.mult).then_inc(bias_scaled, 1)
            dve.tensor_copy(wk_sb[:, :, :, :], wkv_ld[:, 0, :, :].unsqueeze(2).broadcast_to([P, DT, HPG, HD])
                            ).then_inc(wk_repeated, 1)

            def thresholds(n):
                dve.wait_ge(abs_total, n + 1)
                dve.tensor_scalar(thr[:, n, 0:1], atot[:, n:n + 1], 1.0 / (D * F), Q_EPS, ALU.mult,
                                  ALU.add).then_inc(thr_step, 1)
                dve.wait_ge(thr_step, 3 * n + 1)
                dve.tensor_scalar(thr[:, n, 1:2], thr[:, n, 0:1], -0.5, None, ALU.mult).then_inc(thr_step, 1)
                dve.wait_ge(thr_step, 3 * n + 2)
                dve.tensor_scalar(thr[:, n, 0:1], thr[:, n, 0:1], 0.5, None, ALU.mult).then_inc(thr_step, 1)
                dve.wait_ge(thr_step, 3 * n + 3)

            def quantise(n, c):
                q, w = piece((q1, q2, q3)[n], c), piece(stage[n], c)
                dve.tensor_scalar(q, w, thr[:, n, 1:2], None, ALU.is_lt).then_inc(compared, 1)
                dve.wait_ge(compared, n * PIECES + c + 1)
                dve.scalar_tensor_tensor(out=q, in0=w, scalar=thr[:, n, 0:1], in1=q, op0=ALU.is_gt,
                                         op1=ALU.subtract).then_inc(quantised, 1)

            def unit(b, name):
                u = UNITS.index(name)
                n = b * len(UNITS) + u
                if name == "k":
                    dve.wait_ge(b_drained, bin_(b, "k"))
                else:
                    dve.wait_ge(a_drained, ain(b, name))
                dve.wait_ge(lo_done, n)
                stand(dve)
                dve.stream_shuffle(rot[:, 1, :], raw[:, u % 2, :],
                                   [(i + HD // 2) % HD for i in range(HD)]).then_inc(swapped, 1)
                dve.wait_ge(swapped, n + 1)
                dve.tensor_tensor(rot[:, 1, :], rot[:, 1, :], sin_sb[:, :], ALU.mult).then_inc(sin_done, 1)
                dve.wait_ge(sin_done, n + 1)
                dve.wait_ge(cos_done, n + 1)
                dve.tensor_tensor(rot[:, 1, :], rot[:, 0, :], rot[:, 1, :], ALU.add).then_inc(rotated, 1)
                dve.wait_ge(rotated, n + 1)
                if name == "k":
                    dve.tensor_copy(k_st[0:64, :], rot[0:64, 1, :]).then_inc(k_ready, 1)
                    dve.tensor_copy(k_st[64:128, :], rot[64:128, 1, :]).then_inc(hi_done, 1)
                    dve.wait_ge(hi_done, n + 1)
                    dve.tensor_tensor(k_st[64:128, :], rot[64:128, 1, :], k_st[64:128, :].bitcast(F32),
                                      ALU.subtract).then_inc(lo_done, 1)
                else:
                    g = int(name[1:])
                    if g:
                        dve.wait_ge(q_in[g - 1], (b + 1) * 16 * 4 * HPG)
                    else:
                        dve.wait_ge(q_in[HG - 1], b * 16 * 4 * HPG)
                    dve.tensor_copy(hi[:, :], rot[:, 1, :]).then_inc(hi_done, 1)
                    dve.wait_ge(hi_done, n + 1)
                    dve.tensor_tensor(lo[:, :], rot[:, 1, :], hi[:, :].bitcast(F32),
                                      ALU.subtract).then_inc(lo_done, 1)

            def h_low(b, t):
                ps, filled, drained, at = wide(t)
                dve.wait_ge(h_hi, (b - 1) * TT + t + 1)
                dve.scalar_tensor_tensor(out=hT[:, 1, :, t * P:(t + 1) * P],
                                         in0=ps[:, :].rearrange("p (k t) -> p k t", k=DT), scalar=H_SCALE,
                                         in1=hT[:, 0, :, t * P:(t + 1) * P], op0=ALU.mult,
                                         op1=ALU.subtract).then_inc(drained, 1)

            def gate(b, f):
                dve.wait_ge(b_filled, bin_(b, f"up{f}"))
                dve.wait_ge(a_drained, ain(b, f"up{f}"))
                dve.scalar_tensor_tensor(out=b_ps[:, :], in0=th[:, :], scalar=1.0, in1=b_ps[:, :],
                                         op0=ALU.add, op1=ALU.mult).then_inc(gated, 1)

            def g_low(b, f):
                dve.wait_ge(g_hi, (b - 1) * FT + f + 1)
                dve.tensor_tensor(gT[:, 1, f, :], b_ps[:, :], gT[:, 0, f, :], ALU.subtract).then_inc(b_drained, 1)

            def stats(c, ln, t, src):
                n = (c * 2 + ln) * TT + t
                dve.bn_stats(stat[:, ln, t, :], src[:, t, :]).then_inc(stat_done, 1)
                dve.wait_ge(stat_done, n + 1)
                stand(dve)
                dve.bn_aggr(mv[:, ln, t, :], stat[:, ln, t, :]).then_inc(mv_done, 1)

            def norm(c, ln, t, src):
                dve.wait_ge(rstd_done, (c * 2 + ln) * TT + t + 1)
                dve.tensor_scalar(h_sb[:, t, :], src[:, t, :], mv[:, ln, t, 0:1], rstd[:, ln, t:t + 1],
                                  ALU.subtract, ALU.mult).then_inc(normed, 1)

            def ffn_out(b, t):
                ps, filled, drained, at = wide(t)
                dve.wait_ge(filled, at(b, f"dn{t}"))
                dve.scalar_tensor_tensor(out=h_sb[:, t, :], in0=ps[:, :], scalar=1.0 / G_SCALE, in1=h_sb[:, t, :],
                                         op0=ALU.mult, op1=ALU.add).then_inc(drained, 1)
                dve.wait_ge(drained, at(b, f"dn{t}"))
                stats(b - 1, 1, t, h_sb)

            def row_max(b, h, t):
                n = h * TT + t
                dve.wait_ge(scored, b * H * TT + n + 1)
                dve.tensor_reduce(sh_sb[:, n % (2 * SR):n % (2 * SR) + 1], s_ps[n % SR][:, :], AX.X,
                                  ALU.min).then_inc(maxed, 1)

            def move(b, h, k):
                dve.wait_ge(transposed, b * H * TT + h * TT + k + 1)
                if h >= PTR:
                    dve.wait_ge(ctx_filled, b * HG + (h - PTR) // HPG + 1)
                dve.tensor_copy(pt_sb[:, h % PTR, k, :], t_ps[k % 2][:, :]).then_inc(pt_dve, 1)

            def reciprocals(b, g):
                dve.wait_ge(expd, b * H * TT + (g + 1) * HPG * TT)
                hs = slice(g * HPG, (g + 1) * HPG)
                dve.wait_ge(rexp_done, b * HG + g)
                dve.reciprocal(rc[:, hs, :], sums[:, hs, :]).then_inc(recip_done, 1)
                dve.wait_ge(recip_done, b * HG + g + 1)
                dve.tensor_copy(rexp[:, :, :, :], rc[:, hs, :].rearrange("p j t -> p t j").unsqueeze(3)
                                .broadcast_to([P, TT, HPG, HD])).then_inc(rexp_done, 1)

            def normalise(b, g):
                dve.wait_ge(ctx_filled, b * HG + g + 1)
                dve.wait_ge(a_drained, ain(b, f"r{g}"))
                dve.tensor_tensor(cx[:, g, :], c_ps[:, :], rT[:, :], ALU.mult).then_inc(ctx_done, 1)

            def period(b):
                first = isinstance(b, int)
                unit(b, "q0")
                unit(b, "k")
                unit(b, "q1")
                if not first:
                    h_low(b, 0)
                    h_low(b, 1)
                dve.wait_ge(b_filled, bin_(b, "vf"))
                dve.tensor_tensor(v_sb[:, :, :], b_ps[:, 0:TT * HD].rearrange("p (t d) -> p t d", t=TT),
                                  bv_sb[:, :].unsqueeze(1).broadcast_to([P, TT, HD]), ALU.add
                                  ).then_inc(b_drained, 1)
                if not first:
                    h_low(b, 2)
                    h_low(b, 3)
                owed = ""
                for h in range(H + 1):
                    use = BESIDE[h]
                    if first and use[:1] != "q":
                        use = ""
                    if h < H:
                        row_max(b, h, 0)
                        row_max(b, h, 1)
                        row_max(b, h, 2)
                    if h % HPG == 0 and h:
                        reciprocals(b, h // HPG - 1)
                    if owed:
                        g_low(b, int(owed[2:]))
                    owed = use if use[:2] == "up" else ""
                    if h >= 1:
                        move(b, h - 1, 1)
                    if h % HPG == 1 and h > HPG:
                        normalise(b, h // HPG - 1)
                    if h < H:
                        row_max(b, h, 3)
                    if use[:2] == "up":
                        gate(b, int(use[2:]))
                    if h >= 1:
                        move(b, h - 1, 3)
                    if use[:1] == "q":
                        unit(b, use)
                    if use[:2] == "dn":
                        ffn_out(b, int(use[2:]))
                    if first and h in QUANTISE_AT:
                        n, c = divmod(QUANTISE_AT.index(h), PIECES)
                        if c == 0:
                            thresholds(n)
                        quantise(n, c)
                if not first:
                    norm(b - 1, 1, 0, h_sb)
                    norm(b - 1, 1, 1, h_sb)
                    ffn_out(b, 2)
                normalise(b, HG - 1)
                if not first:
                    ffn_out(b, 3)
                    norm(b - 1, 1, 2, h_sb)
                    norm(b - 1, 1, 3, h_sb)
                dve.wait_ge(normed, b * 2 * TT)
                dve.wait_ge(stored, b * TT * 16)
                for t in range(TT):
                    ps, filled, drained, at = wide(t)
                    dve.wait_ge(bo_added, b * TT + t + 1)
                    dve.wait_ge(filled, at(b, f"wo{t}"))
                    dve.tensor_tensor(xb[:, t, :], ps[:, :], xb[:, t, :], ALU.add).then_inc(drained, 1)
                    dve.wait_ge(drained, at(b, f"wo{t}"))
                    stats(b, 0, t, xb)
                    if t:
                        norm(b, 0, t - 1, xb)
                norm(b, 0, TT - 1, xb)

            period(0)
            with dve.Fori(1, B) as b:
                period(b)
            for t in range(TT):
                h_low(B, t)
            for f in range(FT):
                gate(B, f)
                g_low(B, f)
            for t in range(TT):
                ffn_out(B, t)
                if t:
                    norm(B - 1, 1, t - 1, h_sb)
            norm(B - 1, 1, TT - 1, h_sb)

        @block.tensor
        def _(pe):
            pe.wait_ge(w_proj, 16 * 10)
            pe.wait_ge(wk_repeated, 1)
            pe.wait_ge(w_late, 16 * 5)

            def project_q(b, g):
                pe.wait_ge(a_drained, ain(b, f"q{g}") - 1)
                for k in range(DT):
                    mm = pe.matmul(a_ps[:, :], wq_sb[:, k, g * P:(g + 1) * P], xT_sb[:, k, :],
                                   start=(k == 0), stop=(k == DT - 1))
                mm.then_inc(a_filled, 1)

            def turn_h(b, t):
                ps, filled, drained, at = wide(t)
                pe.wait_ge(normed, (b - 1) * 2 * TT + t + 1)
                pe.wait_ge(drained, at(b, f"ht{t}") - 1)
                for k in range(DT):
                    mm = pe.transpose(ps[:, k * P:(k + 1) * P], h_sb[:, t, k * P:(k + 1) * P], id_sb[:, :])
                mm.then_inc(filled, 1)

            def up(b, f, half):
                ps, filled, drained, at = wide(half)
                w = (q1v, q2v)[half]
                if f == 0 and half == 0:
                    pe.wait_ge(b_drained, bin_(b, "ht3"))
                pe.wait_ge(drained, at(b, f"up{f}") - 1)
                for k in range(DT):
                    for s in range(2):
                        mm = pe.matmul(ps[:, :], w[:, k, f * P:(f + 1) * P], hT[:, s, k, :],
                                       start=(k == 0 and s == 0), stop=(k == DT - 1 and s == 1))
                mm.then_inc(filled, 1)

            def down(b, t):
                ps, filled, drained, at = wide(t)
                pe.wait_ge(drained, at(b, f"dn{t}") - 1)
                for f in range(FT):
                    if t == 0:
                        pe.wait_ge(b_drained, bin_(b, f"up{f}"))
                    for s in range(2):
                        mm = pe.matmul(ps[:, :], gT[:, s, f, t * P:(t + 1) * P], q3v[:, f, :],
                                       start=(f == 0 and s == 0), stop=(f == FT - 1 and s == 1))
                mm.then_inc(filled, 1)

            def score(b, h, t):
                n = h * TT + t
                pe.wait_ge(expd, b * H * TT + max(n - SR + 1, 0))
                if n % (HPG * TT) == 0:
                    pe.wait_ge(q_in[h // HPG], (b + 1) * 16 * 4 * HPG)
                if n == 0:
                    pe.wait_ge(lo_done, b * len(UNITS) + UNITS.index("k") + 1)
                pe.matmul(s_ps[n % SR][:, :], q_st[:, h % (QR * HPG), t * P:(t + 1) * P], k_st[:, :],
                          start=True, stop=True).then_inc(scored, 1)

            def turn(b, h, k):
                pe.wait_ge(expd, b * H * TT + (h + 1) * TT)
                if k % 2 == 0:
                    pe.wait_ge(pt_act, b * H * 2 + h * 2 + k // 2)
                else:
                    pe.wait_ge(pt_dve, b * H * 2 + h * 2 + k // 2)
                for t in range(TT):
                    mm = pe.transpose(t_ps[k % 2][:, t * P:(t + 1) * P], p_sb[:, h % 2, t, k * P:(k + 1) * P],
                                      id_sb[:, :])
                mm.then_inc(transposed, 1)

            def context(b, g):
                pe.wait_ge(rexp_done, b * HG + g + 1)
                pe.wait_ge(a_drained, ain(b, f"r{g}") - 1)
                for t in range(TT):
                    mm = pe.transpose(a_ps[:, t * P:(t + 1) * P], rexp[:, t, :, :].rearrange("p j d -> p (j d)"),
                                      id_sb[:, :])
                mm.then_inc(a_filled, 1)
                pe.wait_ge(ctx_done, b * HG + g)
                pe.wait_ge(pt_act, b * H * 2 + (g + 1) * HPG * 2)
                pe.wait_ge(pt_dve, b * H * 2 + (g + 1) * HPG * 2)
                for k in range(TT):
                    for j in range(HPG):
                        mm = pe.matmul(c_ps[HD * j:HD * (j + 1), :], v_sb[:, k, :],
                                       pt_sb[:, (g * HPG + j) % PTR, k, :], start=(k == 0), stop=(k == TT - 1))
                mm.then_inc(ctx_filled, 1)

            def period(b):
                first = isinstance(b, int)
                pe.wait_ge(xT_in, (b + 1) * 16)
                project_q(b, 0)
                pe.wait_ge(b_drained, bin_(b, "k") - 1)
                for k in range(DT):
                    mm = pe.matmul(b_ps[:, :], wk_sb[:, k, :, :].rearrange("p j d -> p (j d)"), xT_sb[:, k, :],
                                   start=(k == 0), stop=(k == DT - 1))
                mm.then_inc(b_filled, 1)
                pe.wait_ge(b_drained, bin_(b, "vp") - 1)
                for k in range(DT):
                    mm = pe.matmul(b_ps[HD * k:HD * (k + 1), :], wkv_ld[:, 1, k, :], xT_sb[:, k, :],
                                   start=True, stop=True)
                mm.then_inc(b_filled, 1)
                project_q(b, 1)
                if not first:
                    turn_h(b, 0)
                    turn_h(b, 1)
                pe.wait_ge(b_drained, bin_(b, "vf") - 1)
                for t in range(TT):
                    mm = pe.matmul(b_ps[:, t * HD:(t + 1) * HD], vp_sb[:, t * P:(t + 1) * P], eye4_sb[:, :],
                                   start=True, stop=True)
                mm.then_inc(b_filled, 1)
                if not first:
                    turn_h(b, 2)
                    turn_h(b, 3)
                for h in range(H + 1):
                    use = BESIDE[h]
                    if first and use[:1] != "q":
                        use = ""
                    if h < H:
                        score(b, h, 0)
                        score(b, h, 1)
                        score(b, h, 2)
                    if h % HPG == 1 and h > HPG:
                        context(b, h // HPG - 1)
                    if use[:2] == "up":
                        up(b, int(use[2:]), 0)
                    if use[:1] == "q":
                        project_q(b, int(use[1:]))
                    if h >= 1:
                        turn(b, h - 1, 0)
                        turn(b, h - 1, 1)
                    if h < H:
                        score(b, h, 3)
                    if use[:2] == "up":
                        up(b, int(use[2:]), 1)
                    if use[:2] == "dn":
                        down(b, int(use[2:]))
                    if h >= 1:
                        turn(b, h - 1, 2)
                        turn(b, h - 1, 3)
                if not first:
                    down(b, 2)
                context(b, HG - 1)
                if not first:
                    down(b, 3)
                for t in range(TT):
                    ps, filled, drained, at = wide(t)
                    pe.wait_ge(drained, at(b, f"wo{t}") - 1)
                    for g in range(HG):
                        if t == 0:
                            pe.wait_ge(ctx_done, b * HG + g + 1)
                        mm = pe.matmul(ps[:, :], cx[:, g, t * P:(t + 1) * P], wo_sb[:, g, :],
                                       start=(g == 0), stop=(g == HG - 1))
                    mm.then_inc(filled, 1)

            period(0)
            pe.wait_ge(quantised, 3 * PIECES)
            with pe.Fori(1, B) as b:
                period(b)
            for t in range(TT):
                turn_h(B, t)
            for f in range(FT):
                up(B, f, 0)
                up(B, f, 1)
            for t in range(TT):
                down(B, t)


def tables():
    f32 = np.float32
    pairs = np.arange(HD // 2, dtype=f32)
    step = (f32(1) / np.power(f32(10000), f32(2) * pairs / f32(HD))).astype(f32)
    angle = (np.arange(T, dtype=f32)[:, None] * step[None, :]).T
    cos, sin = np.cos(angle).astype(f32), np.sin(angle).astype(f32)
    return (np.tile(np.concatenate([cos, cos]), (HPG, 1)), np.tile(np.concatenate([-sin, sin]), (HPG, 1)),
            np.eye(P, dtype=f32), np.tile(np.eye(HD, dtype=f32), (HPG, 1)))


def kernel(L0_attn_x, L0_attn_Wq, L0_attn_bq, L0_attn_Wk, L0_attn_bk, L0_attn_Wv, L0_attn_bv, L0_attn_Wo,
           L0_attn_bo, L0_ffn_w1, L0_ffn_w2, L0_ffn_w3):
    import concourse.bacc as bacc
    from concourse.bass_utils import run_bass_kernel_spmd

    def rows(a, tiles):
        return np.ascontiguousarray(a.reshape(tiles, P, -1).transpose(1, 0, 2).reshape(P, -1))

    x = np.asarray(L0_attn_x)
    cos, sin, ident, eye4 = tables()
    arrays = {
        "xT": np.stack([rows(x[b].T, DT) for b in range(B)]),
        "x": np.ascontiguousarray(x),
        "wq": np.asarray(L0_attn_Wq),
        "wk": rows(np.asarray(L0_attn_Wk), DT),
        "wv": rows(np.asarray(L0_attn_Wv), DT),
        "wo": np.asarray(L0_attn_Wo),
        "bq": np.ascontiguousarray(np.asarray(L0_attn_bq).reshape(HG, P).T),
        "bk": np.asarray(L0_attn_bk).reshape(HD, 1),
        "bv": np.asarray(L0_attn_bv),
        "bo": np.asarray(L0_attn_bo),
        "w1": rows(np.asarray(L0_ffn_w1).T, DT),
        "w2": rows(np.asarray(L0_ffn_w2).T, DT),
        "w3": rows(np.asarray(L0_ffn_w3).T, FT),
        "cos": cos, "sin": sin, "ident": ident, "eye4": eye4,
    }
    nc = bacc.Bacc("TRN2", target_bir_lowering=False, num_devices=1)
    aps = [nc.dram_tensor(f"in_{n}", a.shape, mybir.dt.from_np(a.dtype), kind="ExternalInput").ap()
           for n, a in arrays.items()]
    out = nc.dram_tensor("out", (B, T, D), F32, kind="ExternalOutput").ap()
    layer(nc, *aps, out)
    r = run_bass_kernel_spmd(nc, [{f"in_{n}": a for n, a in arrays.items()}], core_ids=[0])
    return r.results[0]["out"]
```

```python
from contextlib import ExitStack

import numpy as np

import concourse.bass as bass
from concourse import mybir

F32 = mybir.dt.float32
F32R = mybir.dt.float32r
F16 = mybir.dt.float16
ALU = mybir.AluOpType
ACT = mybir.ActivationFunctionType
AX = mybir.AxisListType
RADD = bass.bass_isa.ReduceOp.add

P = 128
B, T, D, H, F = 4, 512, 512, 16, 1408
HD = D // H
DT = D // P
TT = T // P
HG = H * HD // P
HPG = H // HG
FT = F // P
SCALE = float(HD) ** -0.5
LN_EPS = 1e-5
Q_EPS = 1e-8
H_SCALE = 32.0
G_SCALE = 2 * H_SCALE
PTR = HPG
QR = 2
SUMS = 4
PIECES = 8
SR = 3
UNITS = ["q0", "k", "q1", "q2", "q3"]
BESIDE = (["up0", "up1", "up2", "up3", "q2", "up4", "up5", "up6", "q3"]
          + [f"up{f}" for f in range(7, FT)] + ["dn0", "dn1", "dn2", "dn3"])
DOWN_FIRST = 4
DOWN_CUT = 7
ABS_AT = [0, 0, 1, 1, 2, 3, 4, 5, 9, 9, 10, 10]
QUANTISE_AT = [h for h in range(3, 15) for _ in range(2)]


def bank_uses(bank):
    uses = ["q0", "q1", "ht0", "ht2"] if bank == "a" else ["k", "vp", "ht1", "vf", "ht3"]
    for h in range(H + 1):
        if h % HPG == 1 and h > HPG and bank == "a":
            uses.append(f"r{h // HPG - 1}")
        use = BESIDE[h]
        if use[:2] == "up" or (use[:1] == "q" and bank == "a"):
            uses.append(use)
        elif use[:2] == "dn" and (int(use[2:]) % 2 == 0) == (bank == "a"):
            uses.append(use)
    uses += [f"r{HG - 1}", "wo0", "wo2"] if bank == "a" else ["wo1", "wo3"]
    return uses


def at_use(bank, period, use):
    uses = bank_uses(bank)
    early = [u for u in uses if u[:2] not in ("ht", "up", "dn")]
    if isinstance(period, int) and period == 0:
        return early.index(use) + 1
    if isinstance(period, int) and period == B:
        late = [u for u in uses if u[:2] in ("ht", "up", "dn")]
        return len(early) + (B - 1) * len(uses) + late.index(use) + 1
    return len(early) + (period - 1) * len(uses) + uses.index(use) + 1


def layer(nc, xT, x, wq, small, wo, b_rows, w1, w2, w3, table, out):
    with ExitStack() as ctx:
        def sb(name, shape, dt=F32):
            return ctx.enter_context(nc.sbuf_tensor(name, shape, dt))

        def sem(name):
            return ctx.enter_context(nc.semaphore(name))

        wq_sb = sb("wq_sb", [P, DT, D])
        wo_sb = sb("wo_sb", [P, HG, D])
        wk_sb = sb("wk_sb", [P, DT, HPG, HD])
        small_sb = sb("small_sb", [P, 2 * DT * HD + HG + 1])
        q1 = sb("q1", [P, DT * F], F16)
        q2 = sb("q2", [P, DT * F], F16)
        q3 = sb("q3", [P, FT * D], F16)
        b_sb = sb("b_sb", [P, HD + D])
        table_sb = sb("table_sb", [P, 2 * T + P + HD])
        xT_sb = sb("xT_sb", [P, DT, T])
        late = sb("late", [P, FT * T + 3 * DT * T])
        raw = sb("raw", [P, 2, T])
        rot = sb("rot", [P, 2, T])
        th = sb("th", [P, T])
        hi = sb("hi", [P, T], F32R)
        lo = sb("lo", [P, T], F32R)
        q_st = sb("q_st", [P, QR * HPG, T], F32R)
        k_st = sb("k_st", [P, T], F32R)
        v_sb = sb("v_sb", [P, TT, HD])
        p_sb = sb("p_sb", [P, 2, TT, T])
        pt_sb = sb("pt_sb", [P, PTR, TT, T])
        sh_sb = sb("sh_sb", [P, 2 * SR])
        sums = sb("sums", [P, H, TT])
        rc = sb("rc", [P, H, TT])
        rexp = sb("rexp", [P, TT, HPG, HD])
        rT = sb("rT", [P, T])
        cx = sb("cx", [P, HG, T])
        stat = sb("stat", [P, 2, TT, 6])
        mv = sb("mv", [P, 2, TT, 2])
        rstd = sb("rstd", [P, 2, TT])
        nhalf = sb("nhalf", [P, 1])
        asum = sb("asum", [P, 3, SUMS])
        atot = sb("atot", [P, 3, SUMS])
        thr = sb("thr", [P, 3, 2])

        gT = late[:, 0:FT * T].bitcast(F16).rearrange("p (s f t) -> p s f t", s=2, f=FT)
        hT = late[:, FT * T:FT * T + DT * T].bitcast(F16).rearrange("p (s k t) -> p s k t", s=2, k=DT)
        h_sb = late[:, FT * T + DT * T:FT * T + 2 * DT * T].rearrange("p (t d) -> p t d", t=TT)
        xb = late[:, FT * T + 2 * DT * T:FT * T + 3 * DT * T].rearrange("p (t d) -> p t d", t=TT)
        wk_ld = small_sb[:, 0:DT * HD].rearrange("p (k d) -> p k d", k=DT)
        wv_sb = small_sb[:, DT * HD:2 * DT * HD].rearrange("p (k d) -> p k d", k=DT)
        bias = small_sb[:, 2 * DT * HD:]
        bv_sb, bo_sb = b_sb[:, 0:HD], b_sb[:, HD:]
        cos_sb, sin_sb = table_sb[:, 0:T], table_sb[:, T:2 * T]
        id_sb, eye4_sb = table_sb[:, 2 * T:2 * T + P], table_sb[:, 2 * T + P:]
        vp_sb = rexp[:, :, :, :].rearrange("p t j d -> p (t j d)")
        stage = [late[:, n * DT * F:(n + 1) * DT * F] for n in (0, 1, 0)]
        q1v = q1[:, :].rearrange("p (k f) -> p k f", k=DT)
        q2v = q2[:, :].rearrange("p (k f) -> p k f", k=DT)
        q3v = q3[:, :].rearrange("p (f d) -> p f d", f=FT)

        def bank(name):
            return ctx.enter_context(nc.psum_tensor(name, [P, 512], F32))

        s_ps = [bank(f"s_ps{n}") for n in range(SR)]
        t_ps = [bank(f"t_ps{n}") for n in range(2)]
        c_ps = bank("c_ps")
        a_ps = bank("a_ps")
        b_ps = bank("b_ps")

        wq_in = sem("wq_in")
        small_in = sem("small_in")
        table_in = sem("table_in")
        b_in = sem("b_in")
        wo_in = sem("wo_in")
        w_ffn = [sem(f"w_ffn{n}") for n in range(3)]
        abs_summed = sem("abs_summed")
        abs_total = sem("abs_total")
        thr_step = sem("thr_step")
        compared = sem("compared")
        quantised = sem("quantised")
        nhalf_set = sem("nhalf_set")
        bias_scaled = sem("bias_scaled")
        wk_repeated = sem("wk_repeated")
        xT_in = sem("xT_in")
        x_in = sem("x_in")
        bo_added = sem("bo_added")
        a_filled = sem("a_filled")
        a_drained = sem("a_drained")
        b_filled = sem("b_filled")
        b_drained = sem("b_drained")
        cos_done = sem("cos_done")
        swapped = sem("swapped")
        sin_done = sem("sin_done")
        rotated = sem("rotated")
        hi_done = sem("hi_done")
        lo_done = sem("lo_done")
        k_ready = sem("k_ready")
        q_in = [sem(f"q_in{j}") for j in range(HPG)]
        scored = sem("scored")
        maxed = sem("maxed")
        expd = sem("expd")
        transposed = sem("transposed")
        pt_act = sem("pt_act")
        pt_dve = sem("pt_dve")
        recip_done = sem("recip_done")
        rexp_done = sem("rexp_done")
        ctx_filled = sem("ctx_filled")
        ctx_done = sem("ctx_done")
        stat_done = sem("stat_done")
        mv_done = sem("mv_done")
        eps_added = sem("eps_added")
        rstd_done = sem("rstd_done")
        normed = sem("normed")
        h_hi = sem("h_hi")
        h_lo = sem("h_lo")
        gated = sem("gated")
        g_hi = sem("g_hi")
        g_low_done = sem("g_low_done")
        stored = sem("stored")
        stood = sem("stood")

        def stand(engine):
            engine.sem_inc(stood, 1)

        def ain(b, use):
            return at_use("a", b, use)

        def bin_(b, use):
            return at_use("b", b, use)

        def wide(n):
            return (a_ps, a_filled, a_drained, ain) if n % 2 == 0 else (b_ps, b_filled, b_drained, bin_)

        def gated_tile(b, f):
            return raw[:, f % 2, :] if isinstance(b, int) else b_ps[:, :]

        def piece(ap, c, pieces=PIECES):
            return ap[:, c * DT * F // pieces:(c + 1) * DT * F // pieces]

        block = ctx.enter_context(nc.Block())


        @block.sync
        def _(sp):
            sp.dma_start(wq_sb[:, :, :], wq.rearrange("(k p) n -> p k n", p=P)).then_inc(wq_in, 16)

            def stack(b, g):
                sp.wait_ge(hi_done, b * len(UNITS) + UNITS.index(f"q{g}") + 1)
                for j in range(HPG):
                    for r in (0, 2, 1, 3):
                        half = (hi, lo)[r % 2]
                        if j == 0 and r == 1:
                            sp.wait_ge(lo_done, b * len(UNITS) + UNITS.index(f"q{g}") + 1)
                        sp.dma_start(q_st[HD * r:HD * (r + 1), g % QR * HPG + j, :].bitcast(F32),
                                     half[HD * j:HD * (j + 1), :].bitcast(F32)).then_inc(q_in[j], 16)

            def period(b):
                first = isinstance(b, int)
                sp.dma_start(xT_sb[:, :, :].rearrange("p k t -> p (k t)"), xT[b, :, :]).then_inc(xT_in, 16)
                if first:
                    sp.wait_ge(xT_in, 16)
                    sp.dma_start(stage[0][:, 0:DT * F // 2], w1[:, 0:DT * F // 2]).then_inc(w_ffn[0], 16)
                stack(b, 0)
                if first:
                    sp.dma_start(stage[0][:, DT * F // 2:], w1[:, DT * F // 2:]).then_inc(w_ffn[0], 16)
                    sp.dma_start(stage[1], w2).then_inc(w_ffn[1], 16)
                stack(b, 1)
                if first:
                    sp.dma_start(wo_sb[:, :, :], wo.rearrange("(k p) n -> p k n", p=P)).then_inc(wo_in, 16)
                if not first:
                    sp.wait_ge(normed, (b * 2 - 1) * TT)
                    stand(sp)
                    sp.dma_start(xb, x[b, :, :].rearrange("(t p) d -> p t d", p=P)).then_inc(x_in, 16)
                sp.wait_ge(scored, (b * H + HPG) * TT)
                stand(sp)
                stack(b, 2)
                if first:
                    sp.wait_ge(quantised, PIECES)
                    sp.dma_start(stage[2], w3).then_inc(w_ffn[2], 16)
                sp.wait_ge(scored, (b * H + 2 * HPG) * TT)
                stand(sp)
                stack(b, 3)
                if first:
                    sp.wait_ge(quantised, 2 * PIECES)
                    sp.dma_start(xb, x[b, :, :].rearrange("(t p) d -> p t d", p=P)).then_inc(x_in, 16)
                sp.wait_ge(a_filled, ain(b, "q3"))
                stand(sp)

            period(0)
            with sp.Fori(1, B) as b:
                period(b)

        @block.gpsimd
        def _(pool):
            pool.memset(nhalf[:, :], -0.5).then_inc(nhalf_set, 1)
            pool.wait_ge(nhalf_set, 1)

            def cosines(b, name):
                u = UNITS.index(name)
                if name == "k":
                    pool.wait_ge(b_drained, bin_(b, "k"))
                else:
                    pool.wait_ge(a_drained, ain(b, name))
                pool.wait_ge(rotated, b * len(UNITS) + u)
                pool.tensor_tensor(rot[:, 0, :], raw[:, u % 2, :], cos_sb, ALU.mult).then_inc(cos_done, 1)

            def thresholds(n):
                pool.wait_ge(abs_summed, (n + 1) * SUMS)
                pool.partition_all_reduce(atot[:, n, :], asum[:, n, :], P, RADD).then_inc(abs_total, 1)
                pool.wait_ge(abs_total, n + 1)
                pool.tensor_tensor(atot[:, n, 0:2], atot[:, n, 0:2], atot[:, n, 2:4], ALU.add).then_inc(thr_step, 1)
                pool.wait_ge(thr_step, 5 * n + 1)
                pool.tensor_tensor(atot[:, n, 0:1], atot[:, n, 0:1], atot[:, n, 1:2], ALU.add).then_inc(thr_step, 1)
                pool.wait_ge(thr_step, 5 * n + 2)
                pool.tensor_scalar(thr[:, n, 0:1], atot[:, n, 0:1], 1.0 / (D * F), Q_EPS, ALU.mult,
                                   ALU.add).then_inc(thr_step, 1)
                pool.wait_ge(thr_step, 5 * n + 3)
                pool.tensor_scalar(thr[:, n, 1:2], thr[:, n, 0:1], -0.5, None, ALU.mult).then_inc(thr_step, 1)
                pool.wait_ge(thr_step, 5 * n + 4)
                pool.tensor_scalar(thr[:, n, 0:1], thr[:, n, 0:1], 0.5, None, ALU.mult).then_inc(thr_step, 1)
                pool.wait_ge(thr_step, 5 * n + 5)

            def below(n, c):
                pool.tensor_scalar(piece((q1, q2, q3)[n], c), piece(stage[n], c), thr[:, n, 1:2], None,
                                   ALU.is_lt).then_inc(compared, 1)

            def rstds(c, ln):
                for t in range(TT):
                    n = (c * 2 + ln) * TT + t
                    pool.wait_ge(mv_done, n + 1)
                    stand(pool)
                    pool.tensor_scalar(rstd[:, ln, t:t + 1], mv[:, ln, t, 1:2], LN_EPS, None,
                                       ALU.add).then_inc(eps_added, 1)
                    pool.wait_ge(eps_added, n + 1)
                    pool.tensor_tensor(rstd[:, ln, t:t + 1], rstd[:, ln, t:t + 1], nhalf[:, :],
                                       ALU.pow).then_inc(rstd_done, 1)

            def store(c):
                for t in range(TT):
                    pool.wait_ge(normed, (c * 2 + 1) * TT + t + 1)
                    stand(pool)
                    pool.dma_start(out[c, t * P:(t + 1) * P, :], h_sb[:, t, :]).then_inc(stored, 16)

            def period(b):
                first = isinstance(b, int)
                cosines(b, "q0")
                cosines(b, "k")
                cosines(b, "q1")
                if first:
                    thresholds(0)
                    for c in range(PIECES):
                        below(0, c)
                cosines(b, "q2")
                if first:
                    thresholds(1)
                    for c in range(PIECES):
                        below(1, c)
                cosines(b, "q3")
                if first:
                    thresholds(2)
                    for c in range(PIECES):
                        below(2, c)
                pool.wait_ge(x_in, (b + 1) * 16)
                for t in range(TT):
                    pool.tensor_tensor(xb[:, t, :], xb[:, t, :], bo_sb, ALU.add).then_inc(bo_added, 1)
                if not first:
                    rstds(b - 1, 1)
                    store(b - 1)
                rstds(b, 0)

            pool.wait_ge(table_in, 16)
            pool.wait_ge(b_in, 16)
            period(0)
            with pool.Fori(1, B) as b:
                period(b)
            rstds(B - 1, 1)
            store(B - 1)
            pool.wait_ge(stored, B * TT * 16)

        @block.scalar
        def _(act):
            act.dma_start(small_sb[:, :], small).then_inc(small_in, 16)
            act.dma_start(table_sb[:, :], table).then_inc(table_in, 16)
            act.dma_start(b_sb[:, :], b_rows.partition_broadcast(P)).then_inc(b_in, 16)

            def unit(b, name):
                u = UNITS.index(name)
                seen = b * len(UNITS) + max(u - 1, 0)
                act.wait_ge(cos_done, seen)
                act.wait_ge(swapped, seen)
                if name == "k":
                    act.wait_ge(b_filled, bin_(b, name))
                    act.activation(raw[:, u % 2, :], b_ps[:, :], ACT.Identity,
                                   bias=bias[:, HG:HG + 1]).then_inc(b_drained, 1)
                else:
                    g = int(name[1:])
                    act.wait_ge(a_filled, ain(b, name))
                    act.activation(raw[:, u % 2, :], a_ps[:, :], ACT.Identity, bias=bias[:, g:g + 1],
                                   scale=-SCALE).then_inc(a_drained, 1)

            def h_high(b, t):
                ps, filled, drained, at = wide(t)
                act.wait_ge(filled, at(b, f"ht{t}"))
                act.activation(hT[:, 0, :, t * P:(t + 1) * P], ps[:, :].rearrange("p (k t) -> p k t", k=DT),
                               ACT.Copy, scale=H_SCALE).then_inc(h_hi, 1)

            def tanh(b, f):
                act.wait_ge(a_filled, ain(b, f"up{f}"))
                if f and isinstance(b, int):
                    act.wait_ge(b_drained, bin_(b, f"up{f - 1}"))
                elif f:
                    act.wait_ge(gated, (b - 1) * FT + f)
                act.activation(th[:, :], a_ps[:, :], ACT.Tanh, scale=0.5 / H_SCALE).then_inc(a_drained, 1)

            def g_high(b, f):
                if isinstance(b, int):
                    act.wait_ge(b_drained, bin_(b, f"up{f}"))
                else:
                    act.wait_ge(gated, (b - 1) * FT + f + 1)
                act.activation(gT[:, 0, f, :], gated_tile(b, f), ACT.Copy).then_inc(g_hi, 1)

            def exps(b, h, t):
                n = h * TT + t
                act.wait_ge(maxed, b * H * TT + n + 1)
                if t == 0:
                    act.wait_ge(transposed, b * H * TT + max(h - 1, 0) * TT)
                act.activation(p_sb[:, h % 2, t, :], s_ps[n % SR][:, :], ACT.Exp,
                               bias=sh_sb[:, n % (2 * SR):n % (2 * SR) + 1], scale=-1.0,
                               accum_out=sums[:, h, t:t + 1]).then_inc(expd, 1)

            def move(b, h, k):
                act.wait_ge(transposed, b * H * TT + h * TT + k + 1)
                if h >= PTR:
                    act.wait_ge(ctx_filled, b * HG + (h - PTR) // HPG + 1)
                act.activation(pt_sb[:, h % PTR, k, :], t_ps[k % 2][:, :], ACT.Copy).then_inc(pt_act, 1)

            def abs_sum(i):
                n, c = divmod(i, SUMS)
                if c == 0:
                    act.wait_ge(w_ffn[n], 16)
                if i == SUMS // 2:
                    act.wait_ge(w_ffn[n], 32)
                act.activation(piece((q1, q2, q3)[n], c, SUMS), piece(stage[n], c, SUMS), ACT.Abs,
                               accum_out=asum[:, n, c:c + 1]).then_inc(abs_summed, 1)

            def norm_row(b, g):
                act.wait_ge(a_filled, ain(b, f"r{g}"))
                act.wait_ge(ctx_done, b * HG + g)
                act.activation(rT[:, :], a_ps[:, :], ACT.Copy).then_inc(a_drained, 1)

            def period(b):
                first = isinstance(b, int)
                unit(b, "q0")
                unit(b, "k")
                act.wait_ge(b_filled, bin_(b, "vp"))
                act.activation(vp_sb, b_ps[:, :], ACT.Copy).then_inc(b_drained, 1)
                unit(b, "q1")
                if not first:
                    for t in range(TT):
                        h_high(b, t)
                owed = ""
                for h in range(H + 1):
                    use = BESIDE[h]
                    if first and use[:1] != "q":
                        use = ""
                    if owed:
                        g_high(b, int(owed[2:]))
                    if h < H:
                        exps(b, h, 0)
                        exps(b, h, 1)
                    owed = use if use[:2] == "up" else ""
                    if h % HPG == 1 and h > HPG:
                        norm_row(b, h // HPG - 1)
                    if h < H:
                        exps(b, h, 2)
                    if use[:2] == "up":
                        tanh(b, int(use[2:]))
                    if use[:1] == "q":
                        unit(b, use)
                    if h >= 1:
                        move(b, h - 1, 0)
                    if h < H:
                        exps(b, h, 3)
                    if h >= 1:
                        move(b, h - 1, 2)
                    if first and h in ABS_AT:
                        for i in range(ABS_AT.count(h)):
                            abs_sum(ABS_AT.index(h) + i)
                norm_row(b, HG - 1)

            act.wait_ge(bias_scaled, 1)
            period(0)
            with act.Fori(1, B) as b:
                period(b)
            for t in range(TT):
                h_high(B, t)
            for f in range(FT):
                tanh(B, f)
                g_high(B, f)

        @block.vector
        def _(dve):
            dve.wait_ge(small_in, 16)
            dve.tensor_scalar(bias[:, 0:HG], bias[:, 0:HG], -SCALE, None, ALU.mult).then_inc(bias_scaled, 1)
            dve.tensor_copy(wk_sb[:, :, :, :], wk_ld.unsqueeze(2).broadcast_to([P, DT, HPG, HD])
                            ).then_inc(wk_repeated, 1)

            def quantise(n, c):
                q, w = piece((q1, q2, q3)[n], c), piece(stage[n], c)
                dve.wait_ge(compared, n * PIECES + c + 1)
                dve.scalar_tensor_tensor(out=q, in0=w, scalar=thr[:, n, 0:1], in1=q, op0=ALU.is_gt,
                                         op1=ALU.subtract).then_inc(quantised, 1)

            def pairs(b, name):
                u = UNITS.index(name)
                n = b * len(UNITS) + u
                if name == "k":
                    dve.wait_ge(b_drained, bin_(b, "k"))
                else:
                    dve.wait_ge(a_drained, ain(b, name))
                dve.wait_ge(lo_done, n)
                stand(dve)
                dve.stream_shuffle(rot[:, 1, :], raw[:, u % 2, :],
                                   [(i + HD // 2) % HD for i in range(HD)]).then_inc(swapped, 1)
                dve.wait_ge(swapped, n + 1)
                dve.tensor_tensor(rot[:, 1, :], rot[:, 1, :], sin_sb, ALU.mult).then_inc(sin_done, 1)

            def rotate(b, name):
                n = b * len(UNITS) + UNITS.index(name)
                dve.wait_ge(sin_done, n + 1)
                dve.wait_ge(cos_done, n + 1)
                dve.tensor_tensor(rot[:, 1, :], rot[:, 0, :], rot[:, 1, :], ALU.add).then_inc(rotated, 1)

            def halves(b, name):
                n = b * len(UNITS) + UNITS.index(name)
                dve.wait_ge(rotated, n + 1)
                if name == "k":
                    dve.tensor_copy(k_st[0:64, :], rot[0:64, 1, :]).then_inc(k_ready, 1)
                    dve.tensor_copy(k_st[64:128, :], rot[64:128, 1, :]).then_inc(hi_done, 1)
                    dve.wait_ge(hi_done, n + 1)
                    dve.tensor_tensor(k_st[64:128, :], rot[64:128, 1, :], k_st[64:128, :].bitcast(F32),
                                      ALU.subtract).then_inc(lo_done, 1)
                else:
                    g = int(name[1:])
                    for j in range(HPG):
                        dve.wait_ge(q_in[j], (b * HG + g) * 16 * 4)
                    dve.tensor_copy(hi[:, :], rot[:, 1, :]).then_inc(hi_done, 1)
                    dve.wait_ge(hi_done, n + 1)
                    dve.tensor_tensor(lo[:, :], rot[:, 1, :], hi[:, :].bitcast(F32),
                                      ALU.subtract).then_inc(lo_done, 1)

            def h_low(b, t):
                ps, filled, drained, at = wide(t)
                dve.wait_ge(h_hi, (b - 1) * TT + t + 1)
                dve.scalar_tensor_tensor(out=hT[:, 1, :, t * P:(t + 1) * P],
                                         in0=ps[:, :].rearrange("p (k t) -> p k t", k=DT), scalar=H_SCALE,
                                         in1=hT[:, 0, :, t * P:(t + 1) * P], op0=ALU.mult,
                                         op1=ALU.subtract).then_inc(drained, 1)

            def gate(b, f):
                dve.wait_ge(b_filled, bin_(b, f"up{f}"))
                dve.wait_ge(a_drained, ain(b, f"up{f}"))
                if isinstance(b, int):
                    if f >= 2:
                        dve.wait_ge(g_low_done, f - 1)
                    dve.scalar_tensor_tensor(out=raw[:, f % 2, :], in0=th[:, :], scalar=1.0, in1=b_ps[:, :],
                                             op0=ALU.add, op1=ALU.mult).then_inc(b_drained, 1)
                else:
                    dve.scalar_tensor_tensor(out=b_ps[:, :], in0=th[:, :], scalar=1.0, in1=b_ps[:, :],
                                             op0=ALU.add, op1=ALU.mult).then_inc(gated, 1)

            def g_low(b, f):
                dve.wait_ge(g_hi, (b - 1) * FT + f + 1)
                dve.tensor_tensor(gT[:, 1, f, :], gated_tile(b, f), gT[:, 0, f, :], ALU.subtract
                                  ).then_inc(g_low_done if isinstance(b, int) else b_drained, 1)

            def stats(c, ln, t, src):
                n = (c * 2 + ln) * TT + t
                dve.bn_stats(stat[:, ln, t, :], src[:, t, :]).then_inc(stat_done, 1)
                dve.wait_ge(stat_done, n + 1)
                stand(dve)
                dve.bn_aggr(mv[:, ln, t, :], stat[:, ln, t, :]).then_inc(mv_done, 1)

            def norm(c, ln, t, src):
                dve.wait_ge(rstd_done, (c * 2 + ln) * TT + t + 1)
                dve.tensor_scalar(h_sb[:, t, :], src[:, t, :], mv[:, ln, t, 0:1], rstd[:, ln, t:t + 1],
                                  ALU.subtract, ALU.mult).then_inc(normed, 1)

            def ffn_out(b, t):
                ps, filled, drained, at = wide(t)
                dve.wait_ge(filled, at(b, f"dn{t}"))
                dve.scalar_tensor_tensor(out=h_sb[:, t, :], in0=ps[:, :], scalar=1.0 / G_SCALE, in1=h_sb[:, t, :],
                                         op0=ALU.mult, op1=ALU.add).then_inc(drained, 1)
                dve.wait_ge(drained, at(b, f"dn{t}"))
                stats(b - 1, 1, t, h_sb)

            def row_max(b, h, t):
                n = h * TT + t
                dve.wait_ge(scored, b * H * TT + n + 1)
                dve.tensor_reduce(sh_sb[:, n % (2 * SR):n % (2 * SR) + 1], s_ps[n % SR][:, :], AX.X,
                                  ALU.min).then_inc(maxed, 1)

            def move(b, h, k):
                dve.wait_ge(transposed, b * H * TT + h * TT + k + 1)
                if h >= PTR:
                    dve.wait_ge(ctx_filled, b * HG + (h - PTR) // HPG + 1)
                dve.tensor_copy(pt_sb[:, h % PTR, k, :], t_ps[k % 2][:, :]).then_inc(pt_dve, 1)

            def reciprocals(b, g):
                dve.wait_ge(expd, b * H * TT + (g + 1) * HPG * TT)
                hs = slice(g * HPG, (g + 1) * HPG)
                dve.wait_ge(rexp_done, b * HG + g)
                dve.reciprocal(rc[:, hs, :], sums[:, hs, :]).then_inc(recip_done, 1)
                dve.wait_ge(recip_done, b * HG + g + 1)
                dve.tensor_copy(rexp[:, :, :, :], rc[:, hs, :].rearrange("p j t -> p t j").unsqueeze(3)
                                .broadcast_to([P, TT, HPG, HD])).then_inc(rexp_done, 1)

            def normalise(b, g):
                dve.wait_ge(ctx_filled, b * HG + g + 1)
                dve.wait_ge(a_drained, ain(b, f"r{g}"))
                dve.tensor_tensor(cx[:, g, :], c_ps[:, :], rT[:, :], ALU.mult).then_inc(ctx_done, 1)

            def period(b):
                first = isinstance(b, int)
                if first:
                    dve.wait_ge(table_in, 16)
                for name in ("q0", "k"):
                    pairs(b, name)
                    rotate(b, name)
                    halves(b, name)
                if first:
                    dve.wait_ge(b_in, 16)
                else:
                    h_low(b, 0)
                    h_low(b, 1)
                dve.wait_ge(b_filled, bin_(b, "vf"))
                dve.tensor_tensor(v_sb[:, :, :], b_ps[:, 0:TT * HD].rearrange("p (t d) -> p t d", t=TT),
                                  bv_sb.unsqueeze(1).broadcast_to([P, TT, HD]), ALU.add
                                  ).then_inc(b_drained, 1)
                if not first:
                    h_low(b, 2)
                    h_low(b, 3)
                pairs(b, "q1")
                rotate(b, "q1")
                owed = ""
                for h in range(H + 1):
                    use = BESIDE[h]
                    if first and use[:1] != "q":
                        use = ""
                    if h < H:
                        row_max(b, h, 0)
                    if owed:
                        g_low(b, int(owed[2:]))
                    if h and BESIDE[h - 1][:1] == "q":
                        rotate(b, BESIDE[h - 1])
                    if h > 1 and BESIDE[h - 2][:1] == "q":
                        halves(b, BESIDE[h - 2])
                    if h < H:
                        row_max(b, h, 1)
                        row_max(b, h, 2)
                    if h % HPG == 0 and h:
                        reciprocals(b, h // HPG - 1)
                    owed = use if use[:2] == "up" else ""
                    if h >= 1:
                        move(b, h - 1, 1)
                    if h % HPG == 1 and h > HPG:
                        normalise(b, h // HPG - 1)
                    if h < H:
                        row_max(b, h, 3)
                    if use[:2] == "up":
                        gate(b, int(use[2:]))
                    if use[:1] == "q":
                        pairs(b, use)
                    if h == 1:
                        halves(b, "q1")
                    if first and h in QUANTISE_AT:
                        quantise(*divmod(QUANTISE_AT.index(h), PIECES))
                    if not first and BESIDE[h - 1][:2] == "dn" and h:
                        t = int(BESIDE[h - 1][2:])
                        ffn_out(b, t)
                        if t:
                            norm(b - 1, 1, t - 1, h_sb)
                    if h >= 1:
                        move(b, h - 1, 3)
                    if first and h in QUANTISE_AT:
                        quantise(*divmod(QUANTISE_AT.index(h) + 1, PIECES))
                normalise(b, HG - 1)
                if not first:
                    ffn_out(b, TT - 1)
                    norm(b - 1, 1, TT - 2, h_sb)
                    norm(b - 1, 1, TT - 1, h_sb)
                dve.wait_ge(normed, b * 2 * TT)
                for t in range(TT):
                    ps, filled, drained, at = wide(t)
                    dve.wait_ge(bo_added, b * TT + t + 1)
                    dve.wait_ge(filled, at(b, f"wo{t}"))
                    dve.tensor_tensor(xb[:, t, :], ps[:, :], xb[:, t, :], ALU.add).then_inc(drained, 1)
                    dve.wait_ge(drained, at(b, f"wo{t}"))
                    stats(b, 0, t, xb)
                    if t == 1:
                        dve.wait_ge(stored, b * TT * 16)
                    if t:
                        norm(b, 0, t - 1, xb)
                norm(b, 0, TT - 1, xb)

            period(0)
            with dve.Fori(1, B) as b:
                period(b)
            for t in range(TT):
                h_low(B, t)
            for f in range(FT):
                gate(B, f)
                g_low(B, f)
            for t in range(TT):
                ffn_out(B, t)
                if t:
                    norm(B - 1, 1, t - 1, h_sb)
            norm(B - 1, 1, TT - 1, h_sb)

        @block.tensor
        def _(pe):
            pe.wait_ge(wq_in, 16)

            def project_q(b, g):
                pe.wait_ge(a_drained, ain(b, f"q{g}") - 1)
                for k in range(DT):
                    mm = pe.matmul(a_ps[:, :], wq_sb[:, k, g * P:(g + 1) * P], xT_sb[:, k, :],
                                   start=(k == 0), stop=(k == DT - 1))
                mm.then_inc(a_filled, 1)

            def turn_h(b, t):
                ps, filled, drained, at = wide(t)
                pe.wait_ge(normed, (b - 1) * 2 * TT + t + 1)
                pe.wait_ge(drained, at(b, f"ht{t}") - 1)
                for k in range(DT):
                    mm = pe.transpose(ps[:, k * P:(k + 1) * P], h_sb[:, t, k * P:(k + 1) * P], id_sb)
                mm.then_inc(filled, 1)

            def up(b, f, half):
                ps, filled, drained, at = wide(half)
                w = (q1v, q2v)[half]
                if f == 0 and half == 0:
                    pe.wait_ge(b_drained, bin_(b, "ht3"))
                pe.wait_ge(drained, at(b, f"up{f}") - 1)
                for k in range(DT):
                    for s in range(2):
                        mm = pe.matmul(ps[:, :], w[:, k, f * P:(f + 1) * P], hT[:, s, k, :],
                                       start=(k == 0 and s == 0), stop=(k == DT - 1 and s == 1))
                mm.then_inc(filled, 1)

            def down(b, t, tiles=range(FT)):
                ps, filled, drained, at = wide(t)
                if tiles[0] == 0:
                    pe.wait_ge(drained, at(b, f"dn{t}") - 1)
                for f in tiles:
                    if t == 0 and isinstance(b, int):
                        pe.wait_ge(g_low_done, f + 1)
                    elif t == 0:
                        pe.wait_ge(b_drained, bin_(b, f"up{f}"))
                    for s in range(2):
                        mm = pe.matmul(ps[:, :], gT[:, s, f, t * P:(t + 1) * P], q3v[:, f, :],
                                       start=(f == 0 and s == 0), stop=(f == FT - 1 and s == 1))
                if tiles[-1] == FT - 1:
                    mm.then_inc(filled, 1)

            def score(b, h, t):
                n = h * TT + t
                pe.wait_ge(expd, b * H * TT + max(n - SR + 1, 0))
                if t == 0:
                    pe.wait_ge(q_in[h % HPG], (b * HG + h // HPG + 1) * 16 * 4)
                if n == 0:
                    pe.wait_ge(lo_done, b * len(UNITS) + UNITS.index("k") + 1)
                pe.matmul(s_ps[n % SR][:, :], q_st[:, h % (QR * HPG), t * P:(t + 1) * P], k_st[:, :],
                          start=True, stop=True).then_inc(scored, 1)

            def turn(b, h, k):
                pe.wait_ge(expd, b * H * TT + (h + 1) * TT)
                if k % 2 == 0:
                    pe.wait_ge(pt_act, b * H * 2 + h * 2 + k // 2)
                else:
                    pe.wait_ge(pt_dve, b * H * 2 + h * 2 + k // 2)
                for t in range(TT):
                    mm = pe.transpose(t_ps[k % 2][:, t * P:(t + 1) * P], p_sb[:, h % 2, t, k * P:(k + 1) * P],
                                      id_sb)
                mm.then_inc(transposed, 1)

            def context(b, g):
                pe.wait_ge(rexp_done, b * HG + g + 1)
                pe.wait_ge(a_drained, ain(b, f"r{g}") - 1)
                for t in range(TT):
                    mm = pe.transpose(a_ps[:, t * P:(t + 1) * P], rexp[:, t, :, :].rearrange("p j d -> p (j d)"),
                                      id_sb)
                mm.then_inc(a_filled, 1)
                pe.wait_ge(ctx_done, b * HG + g)
                pe.wait_ge(pt_act, b * H * 2 + (g + 1) * HPG * 2)
                pe.wait_ge(pt_dve, b * H * 2 + (g + 1) * HPG * 2)
                for k in range(TT):
                    for j in range(HPG):
                        mm = pe.matmul(c_ps[HD * j:HD * (j + 1), :], v_sb[:, k, :],
                                       pt_sb[:, (g * HPG + j) % PTR, k, :], start=(k == 0), stop=(k == TT - 1))
                mm.then_inc(ctx_filled, 1)

            def period(b):
                first = isinstance(b, int)
                pe.wait_ge(xT_in, (b + 1) * 16)
                project_q(b, 0)
                if first:
                    pe.wait_ge(wk_repeated, 1)
                pe.wait_ge(b_drained, bin_(b, "k") - 1)
                for k in range(DT):
                    mm = pe.matmul(b_ps[:, :], wk_sb[:, k, :, :].rearrange("p j d -> p (j d)"), xT_sb[:, k, :],
                                   start=(k == 0), stop=(k == DT - 1))
                mm.then_inc(b_filled, 1)
                pe.wait_ge(b_drained, bin_(b, "vp") - 1)
                for k in range(DT):
                    mm = pe.matmul(b_ps[HD * k:HD * (k + 1), :], wv_sb[:, k, :], xT_sb[:, k, :],
                                   start=True, stop=True)
                mm.then_inc(b_filled, 1)
                project_q(b, 1)
                if not first:
                    turn_h(b, 0)
                    turn_h(b, 1)
                if first:
                    pe.wait_ge(table_in, 16)
                pe.wait_ge(b_drained, bin_(b, "vf") - 1)
                for t in range(TT):
                    mm = pe.matmul(b_ps[:, t * HD:(t + 1) * HD], vp_sb[:, t * P:(t + 1) * P], eye4_sb,
                                   start=True, stop=True)
                mm.then_inc(b_filled, 1)
                if not first:
                    turn_h(b, 2)
                    turn_h(b, 3)
                for h in range(H + 1):
                    use = BESIDE[h]
                    if first and use[:1] != "q":
                        use = ""
                    if h < H:
                        score(b, h, 0)
                        score(b, h, 1)
                        score(b, h, 2)
                    if h % HPG == 1 and h > HPG:
                        context(b, h // HPG - 1)
                    if use[:2] == "up":
                        up(b, int(use[2:]), 0)
                    if use[:2] == "dn":
                        down(b, int(use[2:]), range(DOWN_FIRST))
                    if use[:1] == "q":
                        project_q(b, int(use[1:]))
                    if h >= 1:
                        turn(b, h - 1, 0)
                        turn(b, h - 1, 1)
                    if h < H:
                        score(b, h, 3)
                    if use[:2] == "up":
                        up(b, int(use[2:]), 1)
                    if use[:2] == "dn":
                        down(b, int(use[2:]), range(DOWN_FIRST, FT if h < H else DOWN_CUT))
                    if h >= 1:
                        turn(b, h - 1, 2)
                        turn(b, h - 1, 3)
                context(b, HG - 1)
                if not first:
                    down(b, TT - 1, range(DOWN_CUT, FT))
                if first:
                    pe.wait_ge(wo_in, 16)
                for t in range(TT):
                    ps, filled, drained, at = wide(t)
                    pe.wait_ge(drained, at(b, f"wo{t}") - 1)
                    for g in range(HG):
                        if t == 0:
                            pe.wait_ge(ctx_done, b * HG + g + 1)
                        mm = pe.matmul(ps[:, :], cx[:, g, t * P:(t + 1) * P], wo_sb[:, g, :],
                                       start=(g == 0), stop=(g == HG - 1))
                    mm.then_inc(filled, 1)

            period(0)
            pe.wait_ge(quantised, 3 * PIECES)
            with pe.Fori(1, B) as b:
                period(b)
            for t in range(TT):
                turn_h(B, t)
            for f in range(FT):
                up(B, f, 0)
                up(B, f, 1)
            for t in range(TT):
                down(B, t)


def table():
    f32 = np.float32
    pairs = np.arange(HD // 2, dtype=f32)
    step = (f32(1) / np.power(f32(10000), f32(2) * pairs / f32(HD))).astype(f32)
    angle = (np.arange(T, dtype=f32)[:, None] * step[None, :]).T
    cos, sin = np.cos(angle).astype(f32), np.sin(angle).astype(f32)
    return np.concatenate([np.tile(np.concatenate([cos, cos]), (HPG, 1)),
                           np.tile(np.concatenate([-sin, sin]), (HPG, 1)),
                           np.eye(P, dtype=f32), np.tile(np.eye(HD, dtype=f32), (HPG, 1))], axis=1)


def kernel(L0_attn_x, L0_attn_Wq, L0_attn_bq, L0_attn_Wk, L0_attn_bk, L0_attn_Wv, L0_attn_bv, L0_attn_Wo,
           L0_attn_bo, L0_ffn_w1, L0_ffn_w2, L0_ffn_w3):
    import concourse.bacc as bacc
    from concourse.bass_utils import run_bass_kernel_spmd

    def rows(a, tiles):
        return np.ascontiguousarray(a.reshape(tiles, P, -1).transpose(1, 0, 2).reshape(P, -1))

    x = np.asarray(L0_attn_x)
    arrays = {
        "xT": np.stack([rows(x[b].T, DT) for b in range(B)]),
        "x": np.ascontiguousarray(x),
        "wq": np.asarray(L0_attn_Wq),
        "small": np.concatenate([rows(np.asarray(L0_attn_Wk), DT), rows(np.asarray(L0_attn_Wv), DT),
                                 np.asarray(L0_attn_bq).reshape(HG, P).T,
                                 np.tile(np.asarray(L0_attn_bk), HPG).reshape(P, 1)], axis=1),
        "wo": np.asarray(L0_attn_Wo),
        "b_rows": np.concatenate([np.asarray(L0_attn_bv), np.asarray(L0_attn_bo)]),
        "w1": rows(np.asarray(L0_ffn_w1).T, DT),
        "w2": rows(np.asarray(L0_ffn_w2).T, DT),
        "w3": rows(np.asarray(L0_ffn_w3).T, FT),
        "table": table(),
    }
    nc = bacc.Bacc("TRN2", target_bir_lowering=False, num_devices=1)
    aps = [nc.dram_tensor(f"in_{n}", a.shape, mybir.dt.from_np(a.dtype), kind="ExternalInput").ap()
           for n, a in arrays.items()]
    out = nc.dram_tensor("out", (B, T, D), F32, kind="ExternalOutput").ap()
    layer(nc, *aps, out)
    r = run_bass_kernel_spmd(nc, [{f"in_{n}": a for n, a in arrays.items()}], core_ids=[0])
    return r.results[0]["out"]
```

```python
from contextlib import ExitStack

import numpy as np

import concourse.bass as bass
from concourse import mybir

F32 = mybir.dt.float32
F32R = mybir.dt.float32r
F16 = mybir.dt.float16
ALU = mybir.AluOpType
ACT = mybir.ActivationFunctionType
AX = mybir.AxisListType
RADD = bass.bass_isa.ReduceOp.add

P = 128
B, T, D, H, F = 4, 512, 512, 16, 1408
HD = D // H
DT = D // P
TT = T // P
HG = H * HD // P
HPG = H // HG
FT = F // P
SCALE = float(HD) ** -0.5
LN_EPS = 1e-5
Q_EPS = 1e-8
H_SCALE = 32.0
G_SCALE = 2 * H_SCALE
PTR = HPG
QR = 2
SUMS = 4
PIECES = 8
SR = 3
UNITS = ["q0", "k", "q1", "q2", "q3"]
BESIDE = (["up0", "up1", "up2", "up3", "q2", "up4", "up5", "up6", "q3"]
          + [f"up{f}" for f in range(7, FT)] + ["dn0", "dn1", "dn2", "dn3"])
FIRST_Q_AT = [3, 7]
DOWN_FIRST = 4
DOWN_CUT = 7
ABS_AT = [0, 0, 1, 1, 2, 3, 4, 5, 9, 9, 10, 10]
QUANTISE_AT = [h for h in list(range(3, 11)) + list(range(12, 16)) for _ in range(2)]


def late_bank(period, use):
    if isinstance(period, int) and period == B:
        return "ab"[int(use[2:]) % 2]
    return "a" if use in ("wo0", "wo2", "wo3") else "b"


def bank_uses(bank, period):
    first = isinstance(period, int) and period == 0
    last = isinstance(period, int) and period == B
    uses = []
    if not last:
        uses += ["q0"] if bank == "a" else ["k"]
    if not first:
        uses += [use for use in [f"{stage}{t}" for stage in ("wo", "ht") for t in range(TT)]
                 if late_bank(period, use) == bank]
    if not last and bank == "a":
        uses += ["q1"]
    for h in range(H + 1):
        use = BESIDE[h]
        if use[:1] == "q" and bank == "a" and not last:
            uses.append(use)
        elif use[:2] == "up" and not first:
            uses.append(use)
        elif use[:2] == "dn" and not first and (int(use[2:]) % 2 == 0) == (bank == "a"):
            uses.append(use)
        if h % HPG == 0 and h and bank == "a" and not last:
            uses.append(f"r{h // HPG - 1}")
    return uses


def at_use(bank, period, use):
    count = bank_uses(bank, period).index(use) + 1
    if isinstance(period, int) and period == 0:
        return count
    return len(bank_uses(bank, 0)) + (period - 1) * len(bank_uses(bank, None)) + count


def layer(nc, xT, x, wq, small, wo, b_rows, w1, w2, w3, table, out):
    with ExitStack() as ctx:
        def sb(name, shape, dt=F32):
            return ctx.enter_context(nc.sbuf_tensor(name, shape, dt))

        def sem(name):
            return ctx.enter_context(nc.semaphore(name))

        wq_sb = sb("wq_sb", [P, DT, D])
        wo_sb = sb("wo_sb", [P, HG, D])
        small_sb = sb("small_sb", [P, 2 * DT * HD + HG + 1])
        q1 = sb("q1", [P, DT * F], F16)
        q2 = sb("q2", [P, DT * F], F16)
        q3 = sb("q3", [P, FT * D], F16)
        b_sb = sb("b_sb", [P, HD + D])
        table_sb = sb("table_sb", [P, 2 * T + 2 * P])
        xT_sb = sb("xT_sb", [P, DT, T])
        late = sb("late", [P, FT * T + 3 * DT * T])
        raw = sb("raw", [P, 2, T])
        rot = sb("rot", [P, 2, T])
        th = sb("th", [P, T])
        hi = sb("hi", [P, T], F32R)
        lo = sb("lo", [P, T], F32R)
        q_st = sb("q_st", [P, QR * HPG, T], F32R)
        k_st = sb("k_st", [P, T], F32R)
        v_sb = sb("v_sb", [P, TT, HD])
        p_sb = sb("p_sb", [P, 2, TT, T])
        pt_sb = sb("pt_sb", [P, PTR, TT, T])
        sh_sb = sb("sh_sb", [P, 2 * SR])
        sums = sb("sums", [P, H, TT])
        rc = sb("rc", [P, H, TT])
        rexp = sb("rexp", [P, TT, HPG, HD])
        rT = sb("rT", [P, T])
        cx = sb("cx", [P, HG, T])
        stat = sb("stat", [P, 2, TT, 6])
        mv = sb("mv", [P, 2, TT, 2])
        rstd = sb("rstd", [P, 2, TT])
        nhalf = sb("nhalf", [P, 1])
        asum = sb("asum", [P, 3, SUMS])
        atot = sb("atot", [P, 3, SUMS])
        thr = sb("thr", [P, 3, 2])

        gT = late[:, 0:FT * T].bitcast(F16).rearrange("p (s f t) -> p s f t", s=2, f=FT)
        hT = late[:, FT * T:FT * T + DT * T].bitcast(F16).rearrange("p (s k t) -> p s k t", s=2, k=DT)
        h_sb = late[:, FT * T + DT * T:FT * T + 2 * DT * T].rearrange("p (t d) -> p t d", t=TT)
        xb = late[:, FT * T + 2 * DT * T:FT * T + 3 * DT * T].rearrange("p (t d) -> p t d", t=TT)
        wk_sb = small_sb[:, 0:DT * HD].rearrange("p (k d) -> p k d", k=DT)
        wv_sb = small_sb[:, DT * HD:2 * DT * HD].rearrange("p (k d) -> p k d", k=DT)
        bias = small_sb[:, 2 * DT * HD:]
        bv_sb, bo_sb = b_sb[:, 0:HD], b_sb[:, HD:]
        cos_sb, sin_sb = table_sb[:, 0:T], table_sb[:, T:2 * T]
        id_sb = table_sb[:, 2 * T:2 * T + P]
        eye4_sb = table_sb[:, 2 * T + P:]
        vp_sb = rexp[:, :, :, :].rearrange("p t j d -> p (t j d)")
        stage = [late[:, n * DT * F:(n + 1) * DT * F] for n in (0, 1, 0)]
        q1v = q1[:, :].rearrange("p (k f) -> p k f", k=DT)
        q2v = q2[:, :].rearrange("p (k f) -> p k f", k=DT)
        q3v = q3[:, :].rearrange("p (f d) -> p f d", f=FT)

        def bank(name):
            return ctx.enter_context(nc.psum_tensor(name, [P, 512], F32))

        s_ps = [bank(f"s_ps{n}") for n in range(SR)]
        t_ps = [bank(f"t_ps{n}") for n in range(2)]
        c_ps = bank("c_ps")
        a_ps = bank("a_ps")
        b_ps = bank("b_ps")

        wq0_in = sem("wq0_in")
        wq_in = sem("wq_in")
        small_in = sem("small_in")
        table_in = sem("table_in")
        b_in = sem("b_in")
        wo_in = sem("wo_in")
        w_ffn = [sem(f"w_ffn{n}") for n in range(3)]
        w1_rest = sem("w1_rest")
        abs_summed = sem("abs_summed")
        abs_total = sem("abs_total")
        thr_step = sem("thr_step")
        compared = sem("compared")
        quantised = sem("quantised")
        nhalf_set = sem("nhalf_set")
        bias_scaled = sem("bias_scaled")
        xT_in = [sem(f"xT_in{n}") for n in range(2)]
        x_in = sem("x_in")
        bo_added = sem("bo_added")
        a_filled = sem("a_filled")
        a_drained = sem("a_drained")
        b_filled = sem("b_filled")
        b_drained = sem("b_drained")
        kv_filled = sem("kv_filled")
        kv_drained = sem("kv_drained")
        cos_done = sem("cos_done")
        swapped = sem("swapped")
        sin_done = sem("sin_done")
        rotated = sem("rotated")
        hi_done = sem("hi_done")
        lo_done = sem("lo_done")
        k_ready = sem("k_ready")
        q_in = [sem(f"q_in{j}") for j in range(HPG)]
        scored = sem("scored")
        maxed = sem("maxed")
        expd = sem("expd")
        transposed = sem("transposed")
        pt_act = sem("pt_act")
        pt_dve = sem("pt_dve")
        recip_done = sem("recip_done")
        rexp_done = sem("rexp_done")
        ctx_filled = sem("ctx_filled")
        ctx_done = sem("ctx_done")
        stat_done = sem("stat_done")
        mv_done = sem("mv_done")
        eps_added = sem("eps_added")
        rstd_done = sem("rstd_done")
        normed = sem("normed")
        h_hi = sem("h_hi")
        gated = sem("gated")
        g_hi = sem("g_hi")
        g_low_done = sem("g_low_done")
        h_free = sem("h_free")
        stood = sem("stood")

        def stand(engine):
            engine.sem_inc(stood, 1)

        def ain(b, use):
            return at_use("a", b, use)

        def bin_(b, use):
            return at_use("b", b, use)

        def wide(n):
            return (a_ps, a_filled, a_drained, ain) if n % 2 == 0 else (b_ps, b_filled, b_drained, bin_)

        def late_tile(b, use):
            return wide(0) if late_bank(b, use) == "a" else wide(1)

        def score_ring(b):
            return SR + 1 if isinstance(b, int) and b == 0 else SR

        def score_bank(b, n):
            return (s_ps + [b_ps])[n % score_ring(b)][:, :]

        def gated_tile(b, f):
            return raw[:, f % 2, :] if isinstance(b, int) else b_ps[:, :]

        def piece(ap, c, pieces=PIECES):
            return ap[:, c * DT * F // pieces:(c + 1) * DT * F // pieces]

        block = ctx.enter_context(nc.Block())


        @block.sync
        def _(sp):
            def stack(b, g):
                sp.wait_ge(hi_done, b * len(UNITS) + UNITS.index(f"q{g}") + 1)
                for j in range(HPG):
                    for r in (0, 2, 1, 3):
                        half = (hi, lo)[r % 2]
                        if j == 0 and r == 1:
                            sp.wait_ge(lo_done, b * len(UNITS) + UNITS.index(f"q{g}") + 1)
                        sp.dma_start(q_st[HD * r:HD * (r + 1), g % QR * HPG + j, :].bitcast(F32),
                                     half[HD * j:HD * (j + 1), :].bitcast(F32)).then_inc(q_in[j], 16)

            def load_xT(b):
                for half in range(2):
                    cols = slice(half * DT * T // 2, (half + 1) * DT * T // 2)
                    sp.dma_start(xT_sb[:, :, :].rearrange("p k t -> p (k t)")[:, cols],
                                 xT[b, :, cols]).then_inc(xT_in[half], 16)

            def store(c, t):
                sp.wait_ge(normed, (c * 2 + 1) * TT + t + 1)
                stand(sp)
                sp.dma_start(out[c, t * P:(t + 1) * P, :], h_sb[:, t, :]).then_inc(h_free, 16)

            def period(b):
                first, last = isinstance(b, int) and b == 0, isinstance(b, int) and b == B - 1
                if first:
                    sp.wait_ge(xT_in[1], 16)
                    sp.dma_start(wq_sb[:, :, P:], wq[:, P:].rearrange("(k p) n -> p k n", p=P)).then_inc(wq_in, 16)
                    sp.dma_start(stage[0][:, 0:DT * F // 2], w1[:, 0:DT * F // 2]).then_inc(w_ffn[0], 16)
                stack(b, 0)
                if first:
                    sp.dma_start(stage[0][:, DT * F // 2:], w1[:, DT * F // 2:]).then_inc(w1_rest, 16)
                    sp.dma_start(stage[1], w2).then_inc(w_ffn[1], 16)
                stack(b, 1)
                if first:
                    sp.dma_start(wo_sb[:, :, :], wo.rearrange("(k p) n -> p k n", p=P)).then_inc(wo_in, 16)
                if not first:
                    sp.wait_ge(normed, (b * 2 - 1) * TT)
                    stand(sp)
                    sp.dma_start(xb, x[b, :, :].rearrange("(t p) d -> p t d", p=P)).then_inc(x_in, 16)
                sp.wait_ge(scored, (b * H + HPG) * TT)
                stand(sp)
                stack(b, 2)
                if first:
                    sp.wait_ge(quantised, PIECES)
                    sp.dma_start(stage[2], w3).then_inc(w_ffn[2], 16)
                sp.wait_ge(scored, (b * H + 2 * HPG) * TT)
                stand(sp)
                stack(b, 3)
                if first:
                    sp.wait_ge(quantised, 2 * PIECES)
                    sp.sem_inc(h_free, 16 * TT)
                    sp.dma_start(xb, x[b, :, :].rearrange("(t p) d -> p t d", p=P)).then_inc(x_in, 16)
                if not last:
                    sp.wait_ge(a_filled, ain(b, "q3"))
                    stand(sp)
                    load_xT(b + 1)
                if not first:
                    for t in range(TT):
                        store(b - 1, t)

            load_xT(0)
            period(0)
            with sp.Fori(1, B - 1) as b:
                period(b)
            period(B - 1)
            for t in range(TT):
                store(B - 1, t)
            sp.wait_ge(h_free, (B + 1) * TT * 16)

        @block.gpsimd
        def _(pool):
            pool.memset(nhalf[:, :], -0.5).then_inc(nhalf_set, 1)
            pool.wait_ge(nhalf_set, 1)

            def cosines(b, name):
                u = UNITS.index(name)
                if name == "k":
                    pool.wait_ge(b_drained, bin_(b, "k"))
                else:
                    pool.wait_ge(a_drained, ain(b, name))
                pool.wait_ge(rotated, b * len(UNITS) + u)
                pool.tensor_tensor(rot[:, 0, :], raw[:, u % 2, :], cos_sb, ALU.mult).then_inc(cos_done, 1)

            def thresholds(n):
                pool.wait_ge(abs_summed, (n + 1) * SUMS)
                pool.partition_all_reduce(atot[:, n, :], asum[:, n, :], P, RADD).then_inc(abs_total, 1)
                pool.wait_ge(abs_total, n + 1)
                pool.tensor_tensor(atot[:, n, 0:2], atot[:, n, 0:2], atot[:, n, 2:4], ALU.add).then_inc(thr_step, 1)
                pool.wait_ge(thr_step, 5 * n + 1)
                pool.tensor_tensor(atot[:, n, 0:1], atot[:, n, 0:1], atot[:, n, 1:2], ALU.add).then_inc(thr_step, 1)
                pool.wait_ge(thr_step, 5 * n + 2)
                pool.tensor_scalar(thr[:, n, 0:1], atot[:, n, 0:1], 1.0 / (D * F), Q_EPS, ALU.mult,
                                   ALU.add).then_inc(thr_step, 1)
                pool.wait_ge(thr_step, 5 * n + 3)
                pool.tensor_scalar(thr[:, n, 1:2], thr[:, n, 0:1], -0.5, None, ALU.mult).then_inc(thr_step, 1)
                pool.wait_ge(thr_step, 5 * n + 4)
                pool.tensor_scalar(thr[:, n, 0:1], thr[:, n, 0:1], 0.5, None, ALU.mult).then_inc(thr_step, 1)
                pool.wait_ge(thr_step, 5 * n + 5)

            def below(n, c):
                pool.tensor_scalar(piece((q1, q2, q3)[n], c), piece(stage[n], c), thr[:, n, 1:2], None,
                                   ALU.is_lt).then_inc(compared, 1)

            def inverse_std(c, ln, t):
                n = (c * 2 + ln) * TT + t
                pool.wait_ge(mv_done, n + 1)
                stand(pool)
                pool.tensor_scalar(rstd[:, ln, t:t + 1], mv[:, ln, t, 1:2], LN_EPS, None,
                                   ALU.add).then_inc(eps_added, 1)
                pool.wait_ge(eps_added, n + 1)
                pool.tensor_tensor(rstd[:, ln, t:t + 1], rstd[:, ln, t:t + 1], nhalf[:, :],
                                   ALU.pow).then_inc(rstd_done, 1)

            def period(b):
                first = isinstance(b, int)
                cosines(b, "q0")
                cosines(b, "k")
                if not first:
                    for t in range(TT):
                        inverse_std(b - 1, 0, t)
                cosines(b, "q1")
                if first:
                    thresholds(0)
                    for c in range(PIECES):
                        below(0, c)
                cosines(b, "q2")
                if first:
                    thresholds(1)
                    for c in range(PIECES):
                        below(1, c)
                cosines(b, "q3")
                if first:
                    thresholds(2)
                    for c in range(PIECES):
                        below(2, c)
                pool.wait_ge(x_in, (b + 1) * 16)
                for t in range(TT):
                    pool.tensor_tensor(xb[:, t, :], xb[:, t, :], bo_sb, ALU.add).then_inc(bo_added, 1)
                if not first:
                    for t in range(TT):
                        inverse_std(b - 1, 1, t)

            pool.wait_ge(table_in, 16)
            pool.wait_ge(b_in, 16)
            period(0)
            with pool.Fori(1, B) as b:
                period(b)
            for ln in range(2):
                for t in range(TT):
                    inverse_std(B - 1, ln, t)

        @block.scalar
        def _(act):
            act.dma_start(wq_sb[:, :, 0:P], wq[:, 0:P].rearrange("(k p) n -> p k n", p=P)).then_inc(wq0_in, 16)
            act.dma_start(small_sb[:, :], small).then_inc(small_in, 16)
            act.dma_start(table_sb[:, :], table).then_inc(table_in, 16)
            act.dma_start(b_sb[:, :], b_rows.partition_broadcast(P)).then_inc(b_in, 16)

            def unit(b, name):
                u = UNITS.index(name)
                seen = b * len(UNITS) + max(u - 1, 0)
                act.wait_ge(cos_done, seen)
                act.wait_ge(swapped, seen)
                if name == "k":
                    act.wait_ge(b_filled, bin_(b, name))
                    act.activation(raw[:, u % 2, :], b_ps[:, :], ACT.Identity,
                                   bias=bias[:, HG:HG + 1]).then_inc(b_drained, 1)
                else:
                    g = int(name[1:])
                    act.wait_ge(a_filled, ain(b, name))
                    act.activation(raw[:, u % 2, :], a_ps[:, :], ACT.Identity, bias=bias[:, g:g + 1],
                                   scale=-SCALE).then_inc(a_drained, 1)

            def h_high(b, t):
                ps, filled, drained, at = late_tile(b, f"ht{t}")
                act.wait_ge(filled, at(b, f"ht{t}"))
                act.activation(hT[:, 0, :, t * P:(t + 1) * P], ps[:, :].rearrange("p (k t) -> p k t", k=DT),
                               ACT.Copy, scale=H_SCALE).then_inc(h_hi, 1)

            def tanh(b, f):
                act.wait_ge(a_filled, ain(b, f"up{f}"))
                if f and isinstance(b, int):
                    act.wait_ge(b_drained, bin_(b, f"up{f - 1}"))
                elif f:
                    act.wait_ge(gated, (b - 1) * FT + f)
                act.activation(th[:, :], a_ps[:, :], ACT.Tanh, scale=0.5 / H_SCALE).then_inc(a_drained, 1)

            def g_high(b, f):
                if isinstance(b, int):
                    act.wait_ge(b_drained, bin_(b, f"up{f}"))
                else:
                    act.wait_ge(gated, (b - 1) * FT + f + 1)
                act.activation(gT[:, 0, f, :], gated_tile(b, f), ACT.Copy).then_inc(g_hi, 1)

            def exps(b, h, t):
                n = h * TT + t
                act.wait_ge(maxed, b * H * TT + n + 1)
                if t == 0:
                    act.wait_ge(transposed, b * H * TT + max(h - 1, 0) * TT)
                act.activation(p_sb[:, h % 2, t, :], score_bank(b, n), ACT.Exp,
                               bias=sh_sb[:, n % (2 * SR):n % (2 * SR) + 1], scale=-1.0,
                               accum_out=sums[:, h, t:t + 1]).then_inc(expd, 1)

            def move(b, h, k):
                act.wait_ge(transposed, b * H * TT + h * TT + k + 1)
                if h >= PTR:
                    act.wait_ge(ctx_filled, b * HG + (h - PTR) // HPG + 1)
                act.activation(pt_sb[:, h % PTR, k, :], t_ps[k % 2][:, :], ACT.Copy).then_inc(pt_act, 1)

            def abs_sum(i):
                n, c = divmod(i, SUMS)
                if c == 0:
                    act.wait_ge(w_ffn[n], 16)
                if i == SUMS // 2:
                    act.wait_ge(w1_rest, 16)
                act.activation(piece((q1, q2, q3)[n], c, SUMS), piece(stage[n], c, SUMS), ACT.Abs,
                               accum_out=asum[:, n, c:c + 1]).then_inc(abs_summed, 1)

            def norm_row(b, g):
                act.wait_ge(a_filled, ain(b, f"r{g}"))
                act.wait_ge(ctx_done, b * HG + g)
                act.activation(rT[:, :], a_ps[:, :], ACT.Copy).then_inc(a_drained, 1)

            def first_heads(b):
                for h in range(H + 1):
                    if h % HPG == 1 and h > HPG:
                        norm_row(b, h // HPG - 1)
                    if h < H:
                        exps(b, h, 0)
                    if h >= 1:
                        move(b, h - 1, 0)
                    if h < H:
                        exps(b, h, 1)
                        exps(b, h, 2)
                    if h >= 1:
                        move(b, h - 1, 2)
                    if h < H:
                        exps(b, h, 3)
                    if h in FIRST_Q_AT:
                        unit(b, f"q{QR + FIRST_Q_AT.index(h)}")
                    if h in ABS_AT:
                        abs_sum(ABS_AT.index(h))
                    if ABS_AT.count(h) == 2:
                        abs_sum(ABS_AT.index(h) + 1)

            def heads(b):
                owed = ""
                for h in range(H + 1):
                    use = BESIDE[h]
                    if owed:
                        g_high(b, int(owed[2:]))
                    owed = use if use[:2] == "up" else ""
                    if 0 < h < H:
                        exps(b, h, 0)
                        exps(b, h, 1)
                        exps(b, h, 2)
                    if h >= 1:
                        move(b, h - 1, 0)
                    if use[:2] == "up":
                        tanh(b, int(use[2:]))
                    if use[:1] == "q":
                        unit(b, use)
                    if h < H:
                        exps(b, h, 3)
                    if h % HPG == 0 and 0 < h < H:
                        norm_row(b, h // HPG - 1)
                    if h >= 1:
                        move(b, h - 1, 2)

            def period(b):
                first = isinstance(b, int)
                unit(b, "q0")
                act.wait_ge(kv_filled, 3 * b + 1)
                act.activation(th[:, :], c_ps[:, :], ACT.Copy).then_inc(kv_drained, 1)
                unit(b, "k")
                act.wait_ge(kv_filled, 3 * b + 2)
                act.activation(vp_sb, c_ps[:, :], ACT.Copy).then_inc(kv_drained, 1)
                if not first:
                    h_high(b, 0)
                    h_high(b, 1)
                    h_high(b, 2)
                    exps(b, 0, 0)
                    exps(b, 0, 1)
                    h_high(b, 3)
                unit(b, "q1")
                if not first:
                    exps(b, 0, 2)
                (first_heads if first else heads)(b)
                norm_row(b, HG - 1)

            act.wait_ge(small_in, 16)
            act.activation(bias[:, 0:HG], bias[:, 0:HG], ACT.Copy, scale=-SCALE).then_inc(bias_scaled, 1)
            act.wait_ge(bias_scaled, 1)
            period(0)
            with act.Fori(1, B) as b:
                period(b)
            for t in range(TT):
                h_high(B, t)
            for f in range(FT):
                tanh(B, f)
                g_high(B, f)

        @block.vector
        def _(dve):
            def quantise(n, c):
                q, w = piece((q1, q2, q3)[n], c), piece(stage[n], c)
                dve.wait_ge(compared, n * PIECES + c + 1)
                dve.scalar_tensor_tensor(out=q, in0=w, scalar=thr[:, n, 0:1], in1=q, op0=ALU.is_gt,
                                         op1=ALU.subtract).then_inc(quantised, 1)

            def pairs(b, name):
                u = UNITS.index(name)
                n = b * len(UNITS) + u
                if name == "k":
                    dve.wait_ge(b_drained, bin_(b, "k"))
                else:
                    dve.wait_ge(a_drained, ain(b, name))
                dve.wait_ge(lo_done, n)
                stand(dve)
                dve.stream_shuffle(rot[:, 1, :], raw[:, u % 2, :],
                                   [(i + HD // 2) % HD for i in range(HD)]).then_inc(swapped, 1)
                dve.wait_ge(swapped, n + 1)
                dve.tensor_tensor(rot[:, 1, :], rot[:, 1, :], sin_sb, ALU.mult).then_inc(sin_done, 1)

            def rotate(b, name):
                n = b * len(UNITS) + UNITS.index(name)
                dve.wait_ge(sin_done, n + 1)
                dve.wait_ge(cos_done, n + 1)
                dve.tensor_tensor(rot[:, 1, :], rot[:, 0, :], rot[:, 1, :], ALU.add).then_inc(rotated, 1)

            def halves(b, name):
                n = b * len(UNITS) + UNITS.index(name)
                dve.wait_ge(rotated, n + 1)
                if name == "k":
                    dve.tensor_copy(k_st[0:64, :], rot[0:64, 1, :]).then_inc(k_ready, 1)
                    dve.tensor_copy(k_st[64:128, :], rot[64:128, 1, :]).then_inc(hi_done, 1)
                    dve.wait_ge(hi_done, n + 1)
                    dve.tensor_tensor(k_st[64:128, :], rot[64:128, 1, :], k_st[64:128, :].bitcast(F32),
                                      ALU.subtract).then_inc(lo_done, 1)
                else:
                    g = int(name[1:])
                    for j in range(HPG):
                        dve.wait_ge(q_in[j], (b * HG + g) * 16 * 4)
                    dve.tensor_copy(hi[:, :], rot[:, 1, :]).then_inc(hi_done, 1)
                    dve.wait_ge(hi_done, n + 1)
                    dve.tensor_tensor(lo[:, :], rot[:, 1, :], hi[:, :].bitcast(F32),
                                      ALU.subtract).then_inc(lo_done, 1)

            def h_low(b, t):
                ps, filled, drained, at = late_tile(b, f"ht{t}")
                dve.wait_ge(h_hi, (b - 1) * TT + t + 1)
                dve.scalar_tensor_tensor(out=hT[:, 1, :, t * P:(t + 1) * P],
                                         in0=ps[:, :].rearrange("p (k t) -> p k t", k=DT), scalar=H_SCALE,
                                         in1=hT[:, 0, :, t * P:(t + 1) * P], op0=ALU.mult,
                                         op1=ALU.subtract).then_inc(drained, 1)

            def gate(b, f):
                dve.wait_ge(b_filled, bin_(b, f"up{f}"))
                dve.wait_ge(a_drained, ain(b, f"up{f}"))
                if isinstance(b, int):
                    if f >= 2:
                        dve.wait_ge(g_low_done, f - 1)
                    dve.scalar_tensor_tensor(out=raw[:, f % 2, :], in0=th[:, :], scalar=1.0, in1=b_ps[:, :],
                                             op0=ALU.add, op1=ALU.mult).then_inc(b_drained, 1)
                else:
                    dve.scalar_tensor_tensor(out=b_ps[:, :], in0=th[:, :], scalar=1.0, in1=b_ps[:, :],
                                             op0=ALU.add, op1=ALU.mult).then_inc(gated, 1)

            def g_low(b, f):
                dve.wait_ge(g_hi, (b - 1) * FT + f + 1)
                dve.tensor_tensor(gT[:, 1, f, :], gated_tile(b, f), gT[:, 0, f, :], ALU.subtract
                                  ).then_inc(g_low_done if isinstance(b, int) else b_drained, 1)

            def stats(c, ln, t, src):
                n = (c * 2 + ln) * TT + t
                dve.bn_stats(stat[:, ln, t, :], src[:, t, :]).then_inc(stat_done, 1)
                dve.wait_ge(stat_done, n + 1)
                stand(dve)
                dve.bn_aggr(mv[:, ln, t, :], stat[:, ln, t, :]).then_inc(mv_done, 1)

            def norm(c, ln, t, src):
                dve.wait_ge(rstd_done, (c * 2 + ln) * TT + t + 1)
                dve.tensor_scalar(h_sb[:, t, :], src[:, t, :], mv[:, ln, t, 0:1], rstd[:, ln, t:t + 1],
                                  ALU.subtract, ALU.mult).then_inc(normed, 1)

            def ffn_out(b, t):
                ps, filled, drained, at = wide(t)
                dve.wait_ge(filled, at(b, f"dn{t}"))
                dve.scalar_tensor_tensor(out=h_sb[:, t, :], in0=ps[:, :], scalar=1.0 / G_SCALE, in1=h_sb[:, t, :],
                                         op0=ALU.mult, op1=ALU.add).then_inc(drained, 1)
                dve.wait_ge(drained, at(b, f"dn{t}"))
                stats(b - 1, 1, t, h_sb)

            def attended(b, t):
                ps, filled, drained, at = late_tile(b, f"wo{t}")
                dve.wait_ge(bo_added, (b - 1) * TT + t + 1)
                dve.wait_ge(filled, at(b, f"wo{t}"))
                dve.tensor_tensor(xb[:, t, :], ps[:, :], xb[:, t, :], ALU.add).then_inc(drained, 1)

            def norm_stats(b, t):
                ps, filled, drained, at = late_tile(b, f"wo{t}")
                dve.wait_ge(drained, at(b, f"wo{t}"))
                stats(b - 1, 0, t, xb)

            def row_max(b, h, t):
                n = h * TT + t
                dve.wait_ge(scored, b * H * TT + n + 1)
                dve.tensor_reduce(sh_sb[:, n % (2 * SR):n % (2 * SR) + 1], score_bank(b, n), AX.X,
                                  ALU.min).then_inc(maxed, 1)

            def move(b, h, k):
                dve.wait_ge(transposed, b * H * TT + h * TT + k + 1)
                if h >= PTR:
                    dve.wait_ge(ctx_filled, b * HG + (h - PTR) // HPG + 1)
                dve.tensor_copy(pt_sb[:, h % PTR, k, :], t_ps[k % 2][:, :]).then_inc(pt_dve, 1)

            def reciprocals(b, g):
                dve.wait_ge(expd, b * H * TT + (g + 1) * HPG * TT)
                hs = slice(g * HPG, (g + 1) * HPG)
                dve.wait_ge(rexp_done, b * HG + g)
                dve.reciprocal(rc[:, hs, :], sums[:, hs, :]).then_inc(recip_done, 1)
                dve.wait_ge(recip_done, b * HG + g + 1)
                dve.tensor_copy(rexp[:, :, :, :], rc[:, hs, :].rearrange("p j t -> p t j").unsqueeze(3)
                                .broadcast_to([P, TT, HPG, HD])).then_inc(rexp_done, 1)

            def normalise(b, g):
                dve.wait_ge(ctx_filled, b * HG + g + 1)
                dve.wait_ge(a_drained, ain(b, f"r{g}"))
                dve.tensor_tensor(cx[:, g, :], c_ps[:, :], rT[:, :], ALU.mult).then_inc(ctx_done, 1)

            def first_heads(b):
                for h in range(H + 1):
                    if h < H:
                        row_max(b, h, 0)
                        row_max(b, h, 1)
                    if h >= 1:
                        move(b, h - 1, 1)
                    if h - 1 in FIRST_Q_AT:
                        pairs(b, f"q{QR + FIRST_Q_AT.index(h - 1)}")
                    if h < H:
                        row_max(b, h, 2)
                    if h % HPG == 0 and h:
                        reciprocals(b, h // HPG - 1)
                    if h < H:
                        row_max(b, h, 3)
                    if h % HPG == 1 and h > HPG:
                        normalise(b, h // HPG - 1)
                    if h in QUANTISE_AT:
                        quantise(*divmod(QUANTISE_AT.index(h), PIECES))
                    if h >= 1:
                        move(b, h - 1, 3)
                    if h - 1 in FIRST_Q_AT:
                        rotate(b, f"q{QR + FIRST_Q_AT.index(h - 1)}")
                        halves(b, f"q{QR + FIRST_Q_AT.index(h - 1)}")
                    if h == 0:
                        pairs(b, "q1")
                        rotate(b, "q1")
                    if h == 1:
                        halves(b, "q1")
                    if h in QUANTISE_AT:
                        quantise(*divmod(QUANTISE_AT.index(h) + 1, PIECES))

            def heads(b):
                owed = ""
                for h in range(H + 1):
                    use = BESIDE[h]
                    if 0 < h < H:
                        row_max(b, h, 0)
                    if owed:
                        g_low(b, int(owed[2:]))
                    owed = use if use[:2] == "up" else ""
                    if h and BESIDE[h - 1][:1] == "q":
                        rotate(b, BESIDE[h - 1])
                    if 0 < h < H:
                        row_max(b, h, 1)
                        row_max(b, h, 2)
                    if h % HPG == 0 and h:
                        reciprocals(b, h // HPG - 1)
                    if h and BESIDE[h - 1][:1] == "q":
                        halves(b, BESIDE[h - 1])
                    if h >= 1:
                        move(b, h - 1, 1)
                    if h % HPG == 1 and h > HPG:
                        normalise(b, h // HPG - 1)
                    if h < H:
                        row_max(b, h, 3)
                    if use[:2] == "up":
                        gate(b, int(use[2:]))
                    if use[:1] == "q":
                        pairs(b, use)
                    if h == 1:
                        halves(b, "q1")
                    if h and BESIDE[h - 1][:2] == "dn":
                        t = int(BESIDE[h - 1][2:])
                        ffn_out(b, t)
                        if t and h < H:
                            norm(b - 1, 1, t - 1, h_sb)
                    if h >= 1:
                        move(b, h - 1, 3)

            def period(b):
                first = isinstance(b, int)
                if first:
                    dve.wait_ge(table_in, 16)
                pairs(b, "q0")
                rotate(b, "q0")
                halves(b, "q0")
                if first:
                    dve.wait_ge(b_in, 16)
                else:
                    attended(b, 0)
                    norm_stats(b, 0)
                pairs(b, "k")
                if not first:
                    dve.wait_ge(h_free, b * TT * 16)
                    norm(b - 1, 0, 0, xb)
                rotate(b, "k")
                halves(b, "k")
                if not first:
                    attended(b, 1)
                    norm_stats(b, 1)
                    attended(b, 2)
                    norm(b - 1, 0, 1, xb)
                    norm_stats(b, 2)
                    h_low(b, 0)
                    norm(b - 1, 0, 2, xb)
                    row_max(b, 0, 0)
                    attended(b, 3)
                    norm_stats(b, 3)
                    h_low(b, 1)
                    row_max(b, 0, 1)
                    norm(b - 1, 0, 3, xb)
                    row_max(b, 0, 2)
                    h_low(b, 2)
                    h_low(b, 3)
                dve.wait_ge(kv_filled, 3 * b + 3)
                dve.tensor_tensor(v_sb[:, :, :], c_ps[:, 0:TT * HD].rearrange("p (t d) -> p t d", t=TT),
                                  bv_sb.unsqueeze(1).broadcast_to([P, TT, HD]), ALU.add
                                  ).then_inc(kv_drained, 1)
                if not first:
                    pairs(b, "q1")
                    rotate(b, "q1")
                (first_heads if first else heads)(b)
                if not first:
                    norm(b - 1, 1, TT - 3, h_sb)
                normalise(b, HG - 1)
                if not first:
                    ffn_out(b, TT - 1)
                    norm(b - 1, 1, TT - 2, h_sb)
                    norm(b - 1, 1, TT - 1, h_sb)
                    dve.wait_ge(normed, b * 2 * TT)

            period(0)
            with dve.Fori(1, B) as b:
                period(b)
            for t in range(TT):
                attended(B, t)
                norm_stats(B, t)
                if t == 0:
                    dve.wait_ge(h_free, B * TT * 16)
                if t:
                    norm(B - 1, 0, t - 1, xb)
            for t in range(TT):
                if t == TT - 2:
                    norm(B - 1, 0, TT - 1, xb)
                h_low(B, t)
            for f in range(FT):
                gate(B, f)
                g_low(B, f)
            for t in range(TT):
                ffn_out(B, t)
                if t:
                    norm(B - 1, 1, t - 1, h_sb)
            norm(B - 1, 1, TT - 1, h_sb)

        @block.tensor
        def _(pe):
            pe.wait_ge(wq0_in, 16)

            def project_q(b, g, tiles=range(DT)):
                if tiles[0] == 0:
                    pe.wait_ge(a_drained, ain(b, f"q{g}") - 1)
                for k in tiles:
                    mm = pe.matmul(a_ps[:, :], wq_sb[:, k, g * P:(g + 1) * P], xT_sb[:, k, :],
                                   start=(k == 0), stop=(k == DT - 1))
                if tiles[-1] == DT - 1:
                    mm.then_inc(a_filled, 1)

            def turn_h(b, t):
                ps, filled, drained, at = late_tile(b, f"ht{t}")
                pe.wait_ge(normed, (b - 1) * 2 * TT + t + 1)
                pe.wait_ge(drained, at(b, f"ht{t}") - 1)
                for k in range(DT):
                    mm = pe.transpose(ps[:, k * P:(k + 1) * P], h_sb[:, t, k * P:(k + 1) * P], id_sb)
                mm.then_inc(filled, 1)

            def project_out(b, t):
                ps, filled, drained, at = late_tile(b, f"wo{t}")
                pe.wait_ge(drained, at(b, f"wo{t}") - 1)
                for g in range(HG):
                    if t == 0:
                        pe.wait_ge(ctx_done, (b - 1) * HG + g + 1)
                    mm = pe.matmul(ps[:, :], cx[:, g, t * P:(t + 1) * P], wo_sb[:, g, :],
                                   start=(g == 0), stop=(g == HG - 1))
                mm.then_inc(filled, 1)

            def up(b, f, half):
                ps, filled, drained, at = wide(half)
                w = (q1v, q2v)[half]
                if f == 0 and half == 0:
                    pe.wait_ge(b_drained, bin_(b, "ht3"))
                pe.wait_ge(drained, at(b, f"up{f}") - 1)
                for k in range(DT):
                    for s in range(2):
                        mm = pe.matmul(ps[:, :], w[:, k, f * P:(f + 1) * P], hT[:, s, k, :],
                                       start=(k == 0 and s == 0), stop=(k == DT - 1 and s == 1))
                mm.then_inc(filled, 1)

            def down(b, t, tiles=range(FT)):
                ps, filled, drained, at = wide(t)
                if tiles[0] == 0:
                    pe.wait_ge(drained, at(b, f"dn{t}") - 1)
                for f in tiles:
                    if t == 0 and isinstance(b, int):
                        pe.wait_ge(g_low_done, f + 1)
                    elif t == 0:
                        pe.wait_ge(b_drained, bin_(b, f"up{f}"))
                    for s in range(2):
                        mm = pe.matmul(ps[:, :], gT[:, s, f, t * P:(t + 1) * P], q3v[:, f, :],
                                       start=(f == 0 and s == 0), stop=(f == FT - 1 and s == 1))
                if tiles[-1] == FT - 1:
                    mm.then_inc(filled, 1)

            def score(b, h, t):
                n = h * TT + t
                pe.wait_ge(expd, b * H * TT + max(n - score_ring(b) + 1, 0))
                if n == SR and score_ring(b) > SR:
                    pe.wait_ge(b_drained, bin_(b, "k"))
                if t == 0:
                    pe.wait_ge(q_in[h % HPG], (b * HG + h // HPG + 1) * 16 * 4)
                if n == 0:
                    pe.wait_ge(lo_done, b * len(UNITS) + UNITS.index("k") + 1)
                pe.matmul(score_bank(b, n), q_st[:, h % (QR * HPG), t * P:(t + 1) * P], k_st[:, :],
                          start=True, stop=True).then_inc(scored, 1)

            def turn(b, h, k):
                pe.wait_ge(expd, b * H * TT + (h + 1) * TT)
                if k % 2 == 0:
                    pe.wait_ge(pt_act, b * H * 2 + h * 2 + k // 2)
                else:
                    pe.wait_ge(pt_dve, b * H * 2 + h * 2 + k // 2)
                for t in range(TT):
                    mm = pe.transpose(t_ps[k % 2][:, t * P:(t + 1) * P], p_sb[:, h % 2, t, k * P:(k + 1) * P],
                                      id_sb)
                mm.then_inc(transposed, 1)

            def parts(w, done):
                for k in range(DT):
                    mm = pe.matmul(c_ps[HD * k:HD * (k + 1), :], w[:, k, :], xT_sb[:, k, :],
                                   start=True, stop=True)
                mm.then_inc(done, 1)

            def key_parts(b):
                pe.wait_ge(ctx_done, b * HG)
                parts(wk_sb, kv_filled)

            def keys(b):
                pe.wait_ge(kv_drained, 3 * b + 1)
                pe.wait_ge(b_drained, bin_(b, "k") - 1)
                pe.matmul(b_ps[:, :], eye4_sb, th[:, :], start=True, stop=True).then_inc(b_filled, 1)

            def value_parts(b):
                pe.wait_ge(kv_drained, 3 * b + 1)
                parts(wv_sb, kv_filled)

            def values(b):
                pe.wait_ge(kv_drained, 3 * b + 2)
                for t in range(TT):
                    mm = pe.matmul(c_ps[:, t * HD:(t + 1) * HD], vp_sb[:, t * P:(t + 1) * P], eye4_sb[:, 0:HD],
                                   start=True, stop=True)
                mm.then_inc(kv_filled, 1)

            def turn_sums(b, g):
                pe.wait_ge(rexp_done, b * HG + g + 1)
                pe.wait_ge(a_drained, ain(b, f"r{g}") - 1)
                for t in range(TT):
                    mm = pe.transpose(a_ps[:, t * P:(t + 1) * P], rexp[:, t, :, :].rearrange("p j d -> p (j d)"),
                                      id_sb)
                mm.then_inc(a_filled, 1)

            def context(b, g):
                if g == 0:
                    pe.wait_ge(kv_drained, 3 * b + 3)
                pe.wait_ge(ctx_done, b * HG + g)
                pe.wait_ge(pt_act, b * H * 2 + (g + 1) * HPG * 2)
                pe.wait_ge(pt_dve, b * H * 2 + (g + 1) * HPG * 2)
                for k in range(TT):
                    for j in range(HPG):
                        mm = pe.matmul(c_ps[HD * j:HD * (j + 1), :], v_sb[:, k, :],
                                       pt_sb[:, (g * HPG + j) % PTR, k, :], start=(k == 0), stop=(k == TT - 1))
                mm.then_inc(ctx_filled, 1)

            def part_of_q(b, h, half):
                for n, at in enumerate(FIRST_Q_AT):
                    if h in (at - 1, at):
                        project_q(b, QR + n, [2 * (h - at + 1) + half])

            def first_heads(b):
                for h in range(H + 1):
                    if h < H:
                        score(b, h, 0)
                        score(b, h, 1)
                        score(b, h, 2)
                        score(b, h, 3)
                    if h % HPG == 1 and h > HPG:
                        context(b, h // HPG - 1)
                    if h >= 1:
                        turn(b, h - 1, 0)
                        turn(b, h - 1, 1)
                    if h < H:
                        part_of_q(b, h, 0)
                    if h >= 1:
                        turn(b, h - 1, 2)
                        turn(b, h - 1, 3)
                    if h < H:
                        part_of_q(b, h, 1)
                    if h % HPG == 0 and h:
                        turn_sums(b, h // HPG - 1)

            def heads(b):
                for h in range(H + 1):
                    use = BESIDE[h]
                    if 0 < h < H:
                        score(b, h, 0)
                        score(b, h, 1)
                        score(b, h, 2)
                    if use[:2] == "up":
                        up(b, int(use[2:]), 0)
                    if use[:2] == "dn":
                        down(b, int(use[2:]), range(DOWN_FIRST))
                    if use[:1] == "q":
                        project_q(b, int(use[1:]))
                    if h % HPG == 1 and h > HPG:
                        context(b, h // HPG - 1)
                    if h >= 1:
                        turn(b, h - 1, 0)
                        turn(b, h - 1, 1)
                    if h < H:
                        score(b, h, 3)
                    if use[:2] == "up":
                        up(b, int(use[2:]), 1)
                    if use[:2] == "dn":
                        down(b, int(use[2:]), range(DOWN_FIRST, FT if h < H else DOWN_CUT))
                    if h >= 1:
                        turn(b, h - 1, 2)
                        turn(b, h - 1, 3)
                    if h % HPG == 0 and h:
                        turn_sums(b, h // HPG - 1)

            def period(b):
                first = isinstance(b, int)
                if first:
                    pe.wait_ge(xT_in[0], 16)
                    project_q(b, 0, [0, 1])
                    pe.wait_ge(xT_in[1], 16)
                    project_q(b, 0, [2, 3])
                    pe.wait_ge(small_in, 16)
                    key_parts(b)
                    pe.wait_ge(wq_in, 16)
                    project_q(b, 1, [0, 1])
                    pe.wait_ge(table_in, 16)
                    keys(b)
                    value_parts(b)
                    project_q(b, 1, [2, 3])
                else:
                    pe.wait_ge(xT_in[0], (b + 1) * 16)
                    pe.wait_ge(xT_in[1], (b + 1) * 16)
                    project_q(b, 0)
                    key_parts(b)
                    project_out(b, 0)
                    keys(b)
                    value_parts(b)
                    project_out(b, 1)
                    project_out(b, 2)
                    turn_h(b, 0)
                    score(b, 0, 0)
                    project_out(b, 3)
                    turn_h(b, 1)
                    score(b, 0, 1)
                    score(b, 0, 2)
                    project_q(b, 1, [0, 1])
                    turn_h(b, 2)
                    project_q(b, 1, [2, 3])
                    turn_h(b, 3)
                values(b)
                (first_heads if first else heads)(b)
                if not first:
                    down(b, TT - 1, range(DOWN_CUT, DOWN_CUT + 2))
                context(b, HG - 1)
                if not first:
                    down(b, TT - 1, range(DOWN_CUT + 2, FT))

            period(0)
            pe.wait_ge(wo_in, 16)
            pe.wait_ge(quantised, 3 * PIECES)
            with pe.Fori(1, B) as b:
                period(b)
            for t in range(TT):
                project_out(B, t)
            for t in range(TT):
                turn_h(B, t)
            for f in range(FT):
                up(B, f, 0)
                up(B, f, 1)
            for t in range(TT):
                down(B, t)


def table():
    f32 = np.float32
    pairs = np.arange(HD // 2, dtype=f32)
    step = (f32(1) / np.power(f32(10000), f32(2) * pairs / f32(HD))).astype(f32)
    angle = (np.arange(T, dtype=f32)[:, None] * step[None, :]).T
    cos, sin = np.cos(angle).astype(f32), np.sin(angle).astype(f32)
    return np.concatenate([np.tile(np.concatenate([cos, cos]), (HPG, 1)),
                           np.tile(np.concatenate([-sin, sin]), (HPG, 1)),
                           np.eye(P, dtype=f32), np.tile(np.eye(HD, dtype=f32), (HPG, HPG))], axis=1)


def kernel(L0_attn_x, L0_attn_Wq, L0_attn_bq, L0_attn_Wk, L0_attn_bk, L0_attn_Wv, L0_attn_bv, L0_attn_Wo,
           L0_attn_bo, L0_ffn_w1, L0_ffn_w2, L0_ffn_w3):
    import concourse.bacc as bacc
    from concourse.bass_utils import run_bass_kernel_spmd

    def rows(a, tiles):
        return np.ascontiguousarray(a.reshape(tiles, P, -1).transpose(1, 0, 2).reshape(P, -1))

    x = np.asarray(L0_attn_x)
    arrays = {
        "xT": np.stack([rows(x[b].T, DT) for b in range(B)]),
        "x": np.ascontiguousarray(x),
        "wq": np.asarray(L0_attn_Wq),
        "small": np.concatenate([rows(np.asarray(L0_attn_Wk), DT), rows(np.asarray(L0_attn_Wv), DT),
                                 np.asarray(L0_attn_bq).reshape(HG, P).T,
                                 np.tile(np.asarray(L0_attn_bk), HPG).reshape(P, 1)], axis=1),
        "wo": np.asarray(L0_attn_Wo),
        "b_rows": np.concatenate([np.asarray(L0_attn_bv), np.asarray(L0_attn_bo)]),
        "w1": rows(np.asarray(L0_ffn_w1).T, DT),
        "w2": rows(np.asarray(L0_ffn_w2).T, DT),
        "w3": rows(np.asarray(L0_ffn_w3).T, FT),
        "table": table(),
    }
    nc = bacc.Bacc("TRN2", target_bir_lowering=False, num_devices=1)
    aps = [nc.dram_tensor(f"in_{n}", a.shape, mybir.dt.from_np(a.dtype), kind="ExternalInput").ap()
           for n, a in arrays.items()]
    out = nc.dram_tensor("out", (B, T, D), F32, kind="ExternalOutput").ap()
    layer(nc, *aps, out)
    r = run_bass_kernel_spmd(nc, [{f"in_{n}": a for n, a in arrays.items()}], core_ids=[0])
    return r.results[0]["out"]
```
